# Optimizing a Trainium2 kernel written in Bass

```python
import numpy as np
import jax
import jax.numpy as jnp

def _softmax(x, axis=-1):
    return jax.nn.softmax(x, axis=axis)

def _gelu(x):
    return jax.nn.gelu(x, approximate=True)

def _silu(x):
    return jax.nn.silu(x)

def _sigmoid(x):
    return jax.nn.sigmoid(x)

def _layernorm(x, axis=-1, eps=1e-05):
    m = jnp.mean(x, axis=axis, keepdims=True)
    v = jnp.var(x, axis=axis, keepdims=True)
    return (x - m) / jnp.sqrt(v + eps)

def _scatter_add(tgt, idx, src, axis=0):
    return tgt.at[idx].add(src)

def _segment_sum(src, seg, n):
    return jax.ops.segment_sum(src, seg, n)
kernel_name = 'mk_prb_d1_jaxref_r8_b86ce2'

def setup_inputs(seed: int=0):
    np.random.seed(seed)
    _w = jnp.asarray

    def _L0_attn_setup():
        import jax, jax.numpy as jnp
        import numpy as np
        LN_EPS = 1e-05
        DENOM_EPS = 1e-06
        NUM_HEADS = 16

        def _layer_norm(x, gamma, beta):
            mu = jnp.mean(x, axis=-1, keepdims=True)
            var = jnp.mean(jnp.square(x - mu), axis=-1, keepdims=True)
            return (x - mu) * jax.lax.rsqrt(var + LN_EPS) * gamma + beta
        key = jax.random.key(seed)
        k1, k2, k3 = jax.random.split(key, 3)
        B, L, D = (4, 512, 128)
        x = jax.random.normal(k1, (B, L, D), dtype=jnp.float32)
        gamma = jnp.ones((D,), dtype=jnp.float32)
        beta = jnp.zeros((D,), dtype=jnp.float32)
        Wqkv = jax.random.normal(k2, (D, 3 * D), dtype=jnp.float32) / np.sqrt(D)
        Wout = jax.random.normal(k3, (D, D), dtype=jnp.float32) / np.sqrt(D)
        return {'x': x, 'gamma': gamma, 'beta': beta, 'Wqkv': Wqkv, 'Wout': Wout}
    _L0_attn_in = _L0_attn_setup()

    def _L0_ffn_setup():
        import jax, jax.numpy as jnp
        import numpy as np
        B, C, D = (2, 256, 128)
        I = 256
        E, K = (8, 2)
        CF = 1.25
        key = jax.random.key(seed)
        k1, k2, k3, k4 = jax.random.split(key, 4)
        scale = 0.02
        return {'hidden_states': jax.random.normal(k1, (B, C, D), jnp.float32), 'Wg': jax.random.normal(k2, (E, D), jnp.float32) * scale, 'W1': jax.random.normal(k3, (E, D, 2 * I), jnp.float32) * scale, 'W2': jax.random.normal(k4, (E, I, D), jnp.float32) * scale}
    _L0_ffn_in = _L0_ffn_setup()
    _d = {'L0_attn_x': _L0_attn_in['x'], 'L0_attn_gamma': _L0_attn_in['gamma'], 'L0_attn_beta': _L0_attn_in['beta'], 'L0_attn_Wqkv': _L0_attn_in['Wqkv'], 'L0_attn_Wout': _L0_attn_in['Wout'], 'L0_ffn_Wg': _L0_ffn_in['Wg'], 'L0_ffn_W1': _L0_ffn_in['W1'], 'L0_ffn_W2': _L0_ffn_in['W2']}
    _x0 = _d['L0_attn_x']
    _d['L0_attn_x'] = jax.random.normal(jax.random.fold_in(jax.random.key(seed), 1), (2, 1024, 128), dtype=_x0.dtype)
    del _x0
    return _d

def reference(L0_attn_x, L0_attn_gamma, L0_attn_beta, L0_attn_Wqkv, L0_attn_Wout, L0_ffn_Wg, L0_ffn_W1, L0_ffn_W2):

    def _L0_attn_ref(x, gamma, beta, Wqkv, Wout):
        import jax, jax.numpy as jnp
        import numpy as np
        LN_EPS = 1e-05
        DENOM_EPS = 1e-06
        NUM_HEADS = 16

        def _layer_norm(x, gamma, beta):
            mu = jnp.mean(x, axis=-1, keepdims=True)
            var = jnp.mean(jnp.square(x - mu), axis=-1, keepdims=True)
            return (x - mu) * jax.lax.rsqrt(var + LN_EPS) * gamma + beta
        B, L, D = x.shape
        H = NUM_HEADS
        HD = D // H
        residual = x
        xn = _layer_norm(x, gamma, beta)
        qkv = (xn @ Wqkv).reshape(B, L, 3, H, HD)
        qkv = jnp.transpose(qkv, (2, 0, 3, 1, 4))
        q, k, v = (qkv[0], qkv[1], qkv[2])
        q = jax.nn.elu(q) + 1.0
        k = jax.nn.elu(k) + 1.0
        kv = jnp.einsum('bhld,bhle->bhde', k, v)
        qkv_out = jnp.einsum('bhld,bhde->bhle', q, kv)
        denom = jnp.einsum('bhld,bhd->bhl', q, k.sum(axis=2)) + DENOM_EPS
        out = qkv_out / denom[..., None]
        out = jnp.transpose(out, (0, 2, 1, 3)).reshape(B, L, D)
        return residual + out @ Wout

    def _L0_ffn_ref(hidden_states, Wg, W1, W2):
        import jax, jax.numpy as jnp
        import numpy as np
        B, C, D = (2, 256, 128)
        I = 256
        E, K = (8, 2)
        CF = 1.25
        Bx, Cx, d = hidden_states.shape
        N = Bx * Cx
        cap = int(N * K * CF / E)
        x = hidden_states.reshape(N, d)
        logits = x @ Wg.T
        top_v, top_i = jax.lax.top_k(logits, K)
        gates = jax.nn.softmax(top_v, axis=-1)
        flat_e = top_i.reshape(N * K)
        gates_f = gates.reshape(N * K)
        tok = jnp.repeat(jnp.arange(N), K)
        onehot = jax.nn.one_hot(flat_e, E, dtype=jnp.int32)
        pos = jnp.cumsum(onehot, axis=0) - 1
        pos_f = jnp.take_along_axis(pos, flat_e[:, None], axis=1)[:, 0]
        keep = pos_f < cap
        pos_safe = jnp.where(keep, pos_f, cap)
        exp_batches = jnp.zeros((E, cap, d), x.dtype).at[flat_e, pos_safe].set(x[tok], mode='drop')
        h = jnp.einsum('ecd,edf->ecf', exp_batches, W1)
        inp, gate = jnp.split(h, 2, axis=-1)
        h = jax.nn.gelu(inp, approximate=False) * gate
        exp_out = jnp.einsum('eci,eid->ecd', h, W2)
        gathered = exp_out[flat_e, jnp.minimum(pos_safe, cap - 1)]
        contrib = jnp.where(keep, gates_f, 0.0)[:, None] * gathered
        out = jax.ops.segment_sum(contrib, tok, num_segments=N)
        return out.reshape(Bx, Cx, d)
    x = L0_attn_x
    xn = _layernorm(x, axis=-1)
    x = x + _L0_attn_ref(xn, L0_attn_gamma, L0_attn_beta, L0_attn_Wqkv, L0_attn_Wout) + _L0_ffn_ref(xn, L0_ffn_Wg, L0_ffn_W1, L0_ffn_W2)
    return x

_drawn_inputs = setup_inputs


def setup_inputs(seed=0):
    import zlib

    import numpy as np

    out = dict(_drawn_inputs(seed))
    spreads = {'L0_attn_gamma': (1.0, 0.6), 'L0_attn_beta': (0.0, 0.492)}
    factors = {'L0_ffn_Wg': 8.0, 'L0_ffn_W1': 8.0, 'L0_ffn_W2': 8.0}
    for name, (base, spread) in spreads.items():
        noise = np.random.default_rng([zlib.crc32(name.encode()), seed]).standard_normal(out[name].shape)
        drawn = base * np.exp(spread * noise) if base else spread * noise
        out[name] = jnp.asarray(drawn.astype(out[name].dtype))
    for name, factor in factors.items():
        out[name] = (out[name] * factor).astype(out[name].dtype)
    return out
```

```python
from contextlib import ExitStack

import concourse.bass as bass
from concourse import mybir

F32 = mybir.dt.float32
F32R = mybir.dt.float32r
F16 = mybir.dt.float16
BF16 = mybir.dt.bfloat16
I32 = mybir.dt.int32
ALU = mybir.AluOpType
ACT = mybir.ActivationFunctionType
AX = mybir.AxisListType

P = 128
LN_EPS = 1e-5
DENOM_EPS = 1e-6
HEADS = 16
TOP_K = 2
CAPACITY_FACTOR = 1.25
GROUP = 4
DENSE = 1
DROPPED = 8192.0
PARTS = ((0, 3), (3, 2))


def moe_attention_block(nc, x, gamma, beta, wqkv, wout, wg_t, w1, w2, out):
    B, L, D = x.shape
    N = B * L
    E, _, F2 = w1.shape
    F = F2 // 2
    T = N // P
    G = T // GROUP
    TB = L // P
    CAP = int(N * TOP_K * CAPACITY_FACTOR / E)
    ST = CAP // P
    R = E - DENSE
    RT = R * ST
    HD = D // HEADS
    FC = F // P
    QKV = 3 * D
    KVW = D + HEADS
    assert D == P and CAP % P == 0 and sum(n for _, n in PARTS) == ST and N <= 2048 and FC == 2

    routed_steps = [(e, j0, nj) for e in range(DENSE, E) for j0, nj in PARTS]
    steps = [(e, j0, nj, r) for r, (e, j0, nj) in enumerate(routed_steps)]
    steps += [(e, g * GROUP, GROUP, None) for e in range(DENSE) for g in range(G)]
    S = len(steps)
    step_of_routed = [s for s in range(S) if steps[s][3] is not None]
    dense_steps = [s for s in range(S) if steps[s][3] is None]
    order_of_experts = list(range(DENSE, E)) + list(range(DENSE))

    x_tiles = x.rearrange("b (t p) d -> p (b t) d", p=P)
    out_tiles = out.rearrange("b (t p) d -> p (b t) d", p=P)
    xn_rows = nc.dram_tensor("xn_rows", [N, D], F32).ap()
    y_rows = nc.dram_tensor("y_rows", [R * CAP, D], F32).ap()
    xn_rows_tiles = xn_rows.rearrange("(t p) d -> p t d", p=P)
    y_rows_tiles = y_rows.rearrange("(t p) d -> p t d", p=P)

    with ExitStack() as ctx:
        def sb(name, shape, dt=F32):
            return ctx.enter_context(nc.sbuf_tensor(name, shape, dt))

        def sem(name):
            return ctx.enter_context(nc.semaphore(name))

        xs = sb("xs", [P, T, D])
        xn = sb("xn", [P, T, D])
        acc = sb("acc", [P, T, D])
        xT_hi = sb("xT_hi", [P, N], F32R)
        xT_lo = sb("xT_lo", [P, N], F32R)
        w1_raw = sb("w1_raw", [P, E, F2])
        w1_hi = sb("w1_hi", [P, E, F2], F32R)
        w1_lo = sb("w1_lo", [P, E, F2], F32R)
        w2_sb = sb("w2_sb", [P, E, FC, D])
        wqkv_sb = sb("wqkv_sb", [P, QKV])
        wqkv_g = sb("wqkv_g", [P, QKV])
        wqkv_hi = sb("wqkv_hi", [P, QKV], F32R)
        wqkv_lo = sb("wqkv_lo", [P, QKV], F32R)
        wout_sb = sb("wout_sb", [P, D])
        wg_sb = sb("wg_sb", [P, E])
        wg_hi = sb("wg_hi", [P, E], F32R)
        wg_lo = sb("wg_lo", [P, E], F32R)
        gamma_sb = sb("gamma_sb", [P, 1])
        beta_sb = sb("beta_sb", [P, 1])
        beta_cols = sb("beta_cols", [P, P])
        bias = sb("bias", [P, QKV])

        ident = sb("ident", [P, P])
        earlier = sb("earlier", [P, P], BF16)
        ones_bf = sb("ones_bf", [P, P], BF16)
        head_block = sb("head_block", [P, D])
        head_cols = sb("head_cols", [P, HEADS])
        iota_p = sb("iota_p", [P, P], F16)
        iota_t = sb("iota_t", [P, RT])
        token_id = sb("token_id", [P, T])
        first_slot = sb("first_slot", [P, T, E])
        rank = sb("rank", [P, T, E])
        eps = sb("eps", [P, 1])

        stats = sb("stats", [P, T, 6])
        mv = sb("mv", [P, T, 2])
        std1 = sb("std1", [P, T])
        inv1 = sb("inv1", [P, T])
        var2 = sb("var2", [P, T])
        std2 = sb("std2", [P, T])
        inv2 = sb("inv2", [P, T])

        logit = sb("logit", [P, T, E])
        rest = sb("rest", [P, T, E])
        eq = sb("eq", [P, T, E])
        chosen = [sb(f"chosen{k}", [P, T, E]) for k in range(TOP_K)]
        top = [sb(f"top{k}", [P, T]) for k in range(TOP_K)]
        best = sb("best", [P, T])
        gap = sb("gap", [P, T])
        gap_exp = sb("gap_exp", [P, T])
        gate_sum = sb("gate_sum", [P, T])
        gate = [sb(f"gate{k}", [P, T]) for k in range(TOP_K)]
        gate_routed = [sb(f"gate_routed{k}", [P, T]) for k in range(TOP_K)]
        assigned = sb("assigned", [P, T, E], BF16)
        kept = sb("kept", [P, T, E])
        slot_all = sb("slot_all", [P, T, E])
        drop = sb("drop", [P, T, E])
        picked = sb("picked", [P, T, E])
        slot = sb("slot", [P, TOP_K, T])
        slot_i = sb("slot_i", [P, TOP_K, T], I32)
        row_i = sb("row_i", [P, TOP_K, T], I32)
        tile_i = sb("tile_i", [P, TOP_K, T], I32)
        row_f = sb("row_f", [P, TOP_K, T])
        kept_routed = sb("kept_routed", [P, TOP_K, T])
        fetch = sb("fetch", [P, TOP_K, T], I32)
        gate_dense = sb("gate_dense", [P, T, E])
        gate_part = sb("gate_part", [P, T, E])
        hot_row = sb("hot_row", [P, TOP_K, T, P], F16)
        hot_tile = sb("hot_tile", [P, TOP_K, T, RT], F16)
        slot_token = sb("slot_token", [P, RT], I32)

        gathered = sb("gathered", [P, RT, D])
        xg_hi = [sb(f"xg_hi{i}", [P, 3 * P], F32R) for i in range(2)]
        xg_lo = [sb(f"xg_lo{i}", [P, 3 * P], F32R) for i in range(2)]
        gelu = [sb(f"gelu{i}", [P, GROUP * P]) for i in range(2)]
        hid = [sb(f"hid{i}", [P, FC, GROUP * P]) for i in range(2)]
        y_sb = [sb(f"y_sb{i}", [P, 3, D]) for i in range(2)]

        pre = [sb(f"pre{i}", [P, QKV + 2]) for i in range(3)]
        expo = [sb(f"expo{i}", [P, 2 * D]) for i in range(2)]
        qk = [sb(f"qk{i}", [P, 2 * D]) for i in range(2)]
        qT = sb("qT", [P, N])
        state = [sb(f"state{b}", [P, KVW]) for b in range(B)]
        den = sb("den", [P, 2, HEADS])
        den_inv = sb("den_inv", [P, 2, HEADS])
        att = [sb(f"att{i}", [P, 2, D]) for i in range(2)]
        attT = [sb(f"attT{i}", [P, 2 * P]) for i in range(2)]
        CR = 8
        fetched = [sb(f"fetched{i}", [P, D]) for i in range(CR)]

        bank_x = [ctx.enter_context(nc.psum_tensor(f"bank_x{i}", [P, 512], F32)) for i in range(2)]
        bank_h = [ctx.enter_context(nc.psum_tensor(f"bank_h{i}", [P, 512], F32)) for i in range(4)]
        bank_y = [ctx.enter_context(nc.psum_tensor(f"bank_y{i}", [P, 512], F32)) for i in range(2)]

        x_in = [sem(f"x_in{g}") for g in range(G)]
        small_in = sem("small_in")
        w_in = [sem(f"w_in{e}") for e in range(E)]
        xn_stored = sem("xn_stored")
        rows_in = [sem(f"rows_in{e}") for e in range(R)]
        y_stored = [sem(f"y_stored{i}") for i in range(2)]
        fetched_in = [sem(f"fetched_in{i}") for i in range(CR)]
        out_stored = sem("out_stored")
        const_ready = sem("const_ready")
        pool_step = sem("pool_step")
        dve_step = sem("dve_step")
        eps_ready = sem("eps_ready")
        mv_ready = sem("mv_ready")
        std1_ready = sem("std1_ready")
        xn_ready = sem("xn_ready")
        xT_raw = sem("xT_raw")
        xT_hi_ready = sem("xT_hi_ready")
        xT_lo_ready = sem("xT_lo_ready")
        wsmall_ready = sem("wsmall_ready")
        logits_ready = sem("logits_ready")
        acc_ready = sem("acc_ready")
        w1_hi_ready = sem("w1_hi_ready")
        w1_lo_ready = sem("w1_lo_ready")
        gap_ready = sem("gap_ready")
        gap_exp_ready = sem("gap_exp_ready")
        assigned_ready = sem("assigned_ready")
        before_ready = sem("before_ready")
        hot_ready = sem("hot_ready")
        slots_ready = sem("slots_ready")
        list_ready = sem("list_ready")
        fetch_ready = sem("fetch_ready")
        gates_ready = sem("gates_ready")
        bias_raw = sem("bias_raw")
        bias_ready = sem("bias_ready")
        var2_ready = sem("var2_ready")
        std2_ready = sem("std2_ready")
        qkv_raw = sem("qkv_raw")
        pre_ready = sem("pre_ready")
        exp_ready = sem("exp_ready")
        qk_ready = sem("qk_ready")
        kv_added = sem("kv_added")
        qT_raw = sem("qT_raw")
        qT_ready = sem("qT_ready")
        state_ready = sem("state_ready")
        att_raw = sem("att_raw")
        att_ready = sem("att_ready")
        attT_raw = sem("attT_raw")
        attT_ready = sem("attT_ready")
        proj_raw = sem("proj_raw")
        proj_added = sem("proj_added")
        xg_raw = sem("xg_raw")
        xg_hi_ready = sem("xg_hi_ready")
        xg_lo_ready = sem("xg_lo_ready")
        up_done = sem("up_done")
        gelu_ready = sem("gelu_ready")
        hid_ready = sem("hid_ready")
        down_done = sem("down_done")
        y_evac = sem("y_evac")
        y_added = sem("y_added")
        fetched_used = sem("fetched_used")

        block = ctx.enter_context(nc.Block())

        def y_freed(eng, s):
            if s < 2:
                return
            r = steps[s - 2][3]
            if r is not None:
                eng.wait_ge(y_evac, r + 1)
            else:
                eng.wait_ge(y_added, dense_steps.index(s - 2) + 1)

        @block.sync
        def _(sp):
            for g in range(G):
                sp.dma_start(xs[:, g * GROUP:(g + 1) * GROUP, :],
                             x_tiles[:, g * GROUP:(g + 1) * GROUP, :]).then_inc(x_in[g], 16)
            for e in order_of_experts:
                sp.dma_start(w1_raw[:, e, :], w1[e]).then_inc(w_in[e], 16)
                sp.dma_start(w2_sb[:, e, :, :],
                             w2[e].rearrange("(c p) d -> p c d", p=P)).then_inc(w_in[e], 16)
            for g in range(G):
                sp.wait_ge(xn_ready, g + 1)
                sp.dma_start(xn_rows_tiles[:, g * GROUP:(g + 1) * GROUP, :],
                             xn[:, g * GROUP:(g + 1) * GROUP, :]).then_inc(xn_stored, 16)
            for r, (e, j0, nj) in enumerate(routed_steps):
                sp.wait_ge(y_evac, r + 1)
                t0 = (e - DENSE) * ST + j0
                sp.dma_start(y_rows_tiles[:, t0:t0 + nj, :],
                             y_sb[r % 2][:, 0:nj, :]).then_inc(y_stored[r % 2], 16)
            for g in range(G):
                sp.wait_ge(fetched_used, (g + 1) * GROUP * TOP_K)
                sp.dma_start(out_tiles[:, g * GROUP:(g + 1) * GROUP, :],
                             acc[:, g * GROUP:(g + 1) * GROUP, :]).then_inc(out_stored, 16)
            sp.wait_ge(out_stored, 16 * G)

        @block.gpsimd
        def _(pool):
            count = [0]

            def link(ins):
                count[0] += 1
                ins.then_inc(pool_step, 1)
                pool.wait_ge(pool_step, count[0])

            link(nc.gpsimd.memset(ident[:], 0.0))
            link(nc.gpsimd.affine_select(out=ident[:], in_=ident[:], compare_op=ALU.not_equal, fill=1.0,
                                         base=0, pattern=[[-1, P]], channel_multiplier=1))
            link(nc.gpsimd.memset(earlier[:], 1.0))
            nc.gpsimd.affine_select(out=earlier[:], in_=earlier[:], compare_op=ALU.is_gt, fill=0.0,
                                    base=0, pattern=[[1, P]], channel_multiplier=-1)
            nc.gpsimd.memset(ones_bf[:], 1.0)
            link(nc.gpsimd.memset(head_cols[:], 1.0))
            link(nc.gpsimd.affine_select(out=head_cols[:], in_=head_cols[:], compare_op=ALU.is_ge, fill=0.0,
                                         base=0, pattern=[[-HD, HEADS]], channel_multiplier=1))
            link(nc.gpsimd.affine_select(out=head_cols[:], in_=head_cols[:], compare_op=ALU.is_ge, fill=0.0,
                                         base=HD - 1, pattern=[[HD, HEADS]], channel_multiplier=-1))
            nc.gpsimd.tensor_copy(head_block[:, :].rearrange("p (h c) -> p h c", h=HEADS),
                                  head_cols[:, :].unsqueeze(2).broadcast_to((P, HEADS, HD)))
            nc.gpsimd.iota(iota_p[:], pattern=[[1, P]], base=0, channel_multiplier=0,
                           allow_small_or_imprecise_dtypes=True)
            nc.gpsimd.iota(iota_t[:], pattern=[[1, RT]], base=0, channel_multiplier=0,
                           allow_small_or_imprecise_dtypes=True)
            nc.gpsimd.iota(token_id[:], pattern=[[P, T]], base=0, channel_multiplier=1,
                           allow_small_or_imprecise_dtypes=True)
            nc.gpsimd.iota(rank[:], pattern=[[0, T], [-1, E]], base=E, channel_multiplier=0,
                           allow_small_or_imprecise_dtypes=True)
            link(nc.gpsimd.memset(first_slot[:], DROPPED))
            link(nc.gpsimd.iota(first_slot[:, :, DENSE:E], pattern=[[0, T], [CAP, R]], base=0,
                                channel_multiplier=0, allow_small_or_imprecise_dtypes=True))
            nc.gpsimd.memset(gap[:], 0.0).then_inc(const_ready, 1)
            for n, e in enumerate(order_of_experts):
                pool.wait_ge(w1_hi_ready, n + 1)
                nc.gpsimd.tensor_tensor(w1_lo[:, e, :], w1_raw[:, e, :], w1_hi[:, e, :].bitcast(F32),
                                        ALU.subtract).then_inc(w1_lo_ready, 1)
                if n % 2 == 1:
                    g = n // 2
                    pool.wait_ge(xn_ready, g + 1)
                    nc.gpsimd.tensor_tensor(acc[:, g * GROUP:(g + 1) * GROUP, :],
                                            xs[:, g * GROUP:(g + 1) * GROUP, :],
                                            xn[:, g * GROUP:(g + 1) * GROUP, :], ALU.add).then_inc(acc_ready, 1)
            pool.wait_ge(xn_stored, 16 * G)
            pool.wait_ge(list_ready, 1)
            for n in range(RT):
                nc.gpsimd.indirect_dma_start(
                    gathered[:, n, :], None, xn_rows,
                    bass.IndirectOffsetOnAxis(ap=slot_token[:, n:n + 1], axis=0),
                ).then_inc(rows_in[n // ST], 16)
            for i in range(2):
                pool.wait_ge(y_stored[i], 16 * len(range(i, len(routed_steps), 2)))
            pool.wait_ge(fetch_ready, 1)
            for n in range(T * TOP_K):
                t, k = n // TOP_K, n % TOP_K
                if n >= CR:
                    pool.wait_ge(fetched_used, n - CR + 1)
                nc.gpsimd.indirect_dma_start(
                    fetched[n % CR][:, :], None, y_rows,
                    bass.IndirectOffsetOnAxis(ap=fetch[:, k, t:t + 1], axis=0),
                ).then_inc(fetched_in[n % CR], 16)

        @block.scalar
        def _(act):
            act.dma_start(wqkv_sb[:, :], wqkv).then_inc(small_in, 16)
            act.dma_start(wg_sb[:, :], wg_t).then_inc(small_in, 16)
            act.dma_start(gamma_sb[:, :], gamma).then_inc(small_in, 16)
            act.dma_start(beta_sb[:, :], beta).then_inc(small_in, 16)
            act.dma_start(wout_sb[:, :], wout).then_inc(small_in, 16)
            act.wait_ge(eps_ready, 1)

            def w1_upper(n):
                e = order_of_experts[n]
                act.wait_ge(w_in[e], 32)
                nc.scalar.activation(w1_hi[:, e, :], w1_raw[:, e, :], ACT.Copy).then_inc(w1_hi_ready, 1)

            for g in range(G):
                t0, t1 = g * GROUP, (g + 1) * GROUP
                act.wait_ge(mv_ready, g + 1)
                nc.scalar.activation(std1[:, t0:t1], mv[:, t0:t1, 1], ACT.Sqrt,
                                     bias=eps[:, 0:1]).then_inc(std1_ready, 1)
                act.wait_ge(xT_raw, g + 1)
                nc.scalar.activation(xT_hi[:, t0 * P:t1 * P], bank_x[g % 2][:, :],
                                     ACT.Copy).then_inc(xT_hi_ready, 1)
            act.wait_ge(var2_ready, 1)
            nc.scalar.activation(std2[:, :], var2[:, :], ACT.Sqrt, bias=eps[:, 0:1]).then_inc(std2_ready, 1)
            for n in range(E):
                w1_upper(n)
            act.wait_ge(gap_ready, 1)
            nc.scalar.activation(gap_exp[:, :], gap[:, :], ACT.Exp).then_inc(gap_exp_ready, 1)
            act.wait_ge(bias_raw, 1)
            nc.scalar.activation(bias[:, :], bank_y[1][:, 0:QKV], ACT.Copy).then_inc(bias_ready, 1)
            for t in range(T):
                act.wait_ge(pre_ready, t + 1)
                if t >= 2:
                    act.wait_ge(qk_ready, t - 1)
                nc.scalar.activation(expo[t % 2][:, :], pre[t % 3][:, 0:2 * D], ACT.Exp).then_inc(exp_ready, 1)
                if t % GROUP == 0 and t > 0:
                    act.wait_ge(qT_raw, t // GROUP)
                    g = t // GROUP - 1
                    nc.scalar.activation(qT[:, g * 512:(g + 1) * 512], bank_x[g % 2][:, :],
                                         ACT.Copy).then_inc(qT_ready, 1)
            act.wait_ge(qT_raw, G)
            nc.scalar.activation(qT[:, (G - 1) * 512:G * 512], bank_x[(G - 1) % 2][:, :],
                                 ACT.Copy).then_inc(qT_ready, 1)
            for u in range(T // 2):
                act.wait_ge(attT_raw, u + 1)
                if u >= 2:
                    act.wait_ge(proj_raw, u - 1)
                nc.scalar.activation(attT[u % 2][:, :], bank_x[u % 2][:, 0:2 * P],
                                     ACT.Copy).then_inc(attT_ready, 1)

            def split_gathered(s):
                r = steps[s][3]
                cols = steps[s][2] * P
                act.wait_ge(xg_raw, r + 1)
                if r >= 2:
                    act.wait_ge(up_done, FC * (step_of_routed[r - 2] + 1))
                nc.scalar.activation(xg_hi[r % 2][:, 0:cols], bank_x[r % 2][:, 0:cols],
                                     ACT.Copy).then_inc(xg_hi_ready, 1)

            def evacuate(s):
                r = steps[s][3]
                if r is None:
                    return
                nj = steps[s][2]
                act.wait_ge(down_done, s + 1)
                if r >= 2:
                    act.wait_ge(y_stored[r % 2], 16 * (r // 2))
                nc.scalar.activation(y_sb[r % 2][:, 0:nj, :],
                                     bank_y[s % 2][:, 0:nj * P].rearrange("p (j d) -> p j d", d=D),
                                     ACT.Copy).then_inc(y_evac, 1)

            if steps[0][3] is not None:
                split_gathered(0)
            for s in range(S):
                cols = steps[s][2] * P
                for c in range(FC):
                    i = FC * s + c
                    act.wait_ge(up_done, i + 1)
                    if i >= 2:
                        act.wait_ge(hid_ready, i - 1)
                    nc.scalar.activation(gelu[i % 2][:, 0:cols], bank_h[2 * c][:, 0:cols],
                                         ACT.Gelu).then_inc(gelu_ready, 1)
                if s + 1 < S and steps[s + 1][3] is not None:
                    split_gathered(s + 1)
                if s >= 1:
                    evacuate(s - 1)
            evacuate(S - 1)

        @block.vector
        def _(dve):
            count = [0]

            def link(ins):
                count[0] += 1
                ins.then_inc(dve_step, 1)
                dve.wait_ge(dve_step, count[0])

            nc.vector.memset(eps[:], LN_EPS).then_inc(eps_ready, 1)
            for i in range(3):
                nc.vector.memset(pre[i][:, QKV:QKV + 2], 1.0)

            def halve_transposed(g):
                dve.wait_ge(xT_hi_ready, g + 1)
                nc.vector.tensor_tensor(xT_lo[:, g * 512:(g + 1) * 512], bank_x[g % 2][:, :],
                                        xT_hi[:, g * 512:(g + 1) * 512].bitcast(F32),
                                        ALU.subtract).then_inc(xT_lo_ready, 1)

            for g in range(G):
                t0, t1 = g * GROUP, (g + 1) * GROUP
                dve.wait_ge(x_in[g], 16)
                for t in range(t0, t1):
                    ins = nc.vector.bn_stats(stats[:, t, :], xs[:, t, :])
                link(ins)
                for t in range(t0, t1):
                    ins = nc.vector.bn_aggr(mv[:, t, :], stats[:, t, :])
                ins.then_inc(mv_ready, 1)
                if g == 0:
                    dve.wait_ge(small_in, 16 * 5)
                    link(nc.vector.tensor_scalar(wqkv_g[:, :], wqkv_sb[:, :], gamma_sb[:, 0:1], None, ALU.mult))
                    nc.vector.tensor_copy(wqkv_hi[:, :], wqkv_g[:, :])
                    link(nc.vector.tensor_copy(wg_hi[:, :], wg_sb[:, :]))
                    nc.vector.tensor_copy(beta_cols[:, :], beta_sb[:, 0:1].broadcast_to((P, P)))
                    nc.vector.tensor_tensor(wqkv_lo[:, :], wqkv_g[:, :], wqkv_hi[:, :].bitcast(F32), ALU.subtract)
                    nc.vector.tensor_tensor(wg_lo[:, :], wg_sb[:, :], wg_hi[:, :].bitcast(F32),
                                            ALU.subtract).then_inc(wsmall_ready, 1)
                dve.wait_ge(std1_ready, g + 1)
                link(nc.vector.reciprocal(inv1[:, t0:t1], std1[:, t0:t1]))
                for t in range(t0, t1):
                    ins = nc.vector.tensor_scalar(xn[:, t, :], xs[:, t, :], mv[:, t, 0:1], inv1[:, t:t + 1],
                                                  ALU.subtract, ALU.mult)
                ins.then_inc(xn_ready, 1)
                if g >= 1:
                    halve_transposed(g - 1)
            halve_transposed(G - 1)
            link(nc.vector.tensor_tensor(var2[:, :], mv[:, :, 1], inv1[:, :], ALU.mult))
            nc.vector.tensor_tensor(var2[:, :], var2[:, :], inv1[:, :], ALU.mult).then_inc(var2_ready, 1)

            def over_experts(ap):
                return ap.unsqueeze(2).broadcast_to((P, T, E))

            dve.wait_ge(const_ready, 1)
            dve.wait_ge(logits_ready, 1)
            link(nc.vector.tensor_copy(logit[:, :, :], bank_y[0][:, 0:T * E].rearrange("p (t e) -> p t e", e=E)))
            scores = logit
            for k in range(TOP_K):
                link(nc.vector.tensor_reduce(top[k][:, :], scores[:, :, :], AX.X, ALU.max))
                link(nc.vector.tensor_tensor(eq[:, :, :], scores[:, :, :], over_experts(top[k][:, :]), ALU.is_equal))
                link(nc.vector.tensor_tensor(eq[:, :, :], eq[:, :, :], rank[:, :, :], ALU.mult))
                link(nc.vector.tensor_reduce(best[:, :], eq[:, :, :], AX.X, ALU.max))
                link(nc.vector.tensor_tensor(chosen[k][:, :, :], eq[:, :, :], over_experts(best[:, :]), ALU.is_equal))
                if k == 0:
                    link(nc.vector.scalar_tensor_tensor(rest[:, :, :], chosen[0][:, :, :], -3e38, logit[:, :, :],
                                                        ALU.mult, ALU.add))
                    scores = rest
            nc.vector.tensor_tensor(assigned[:, :, :], chosen[0][:, :, :], chosen[1][:, :, :],
                                    ALU.add).then_inc(assigned_ready, 1)
            nc.vector.tensor_tensor(gap[:, :], top[1][:, :], top[0][:, :], ALU.subtract).then_inc(gap_ready, 1)
            dve.wait_ge(before_ready, 1)
            before = bank_y[0][:, 128:128 + T * E].rearrange("p (t e) -> p t e", e=E)
            nc.vector.tensor_scalar(drop[:, :, :], before, float(CAP), DROPPED, ALU.is_ge, ALU.mult)
            nc.vector.tensor_scalar(kept[:, :, :], before, float(CAP), None, ALU.is_lt)
            link(nc.vector.tensor_tensor(slot_all[:, :, :], before, first_slot[:, :, :], ALU.add))
            link(nc.vector.tensor_tensor(slot_all[:, :, :], slot_all[:, :, :], drop[:, :, :], ALU.add))
            for k in range(TOP_K):
                link(nc.vector.tensor_tensor(picked[:, :, :], slot_all[:, :, :], chosen[k][:, :, :], ALU.mult))
                link(nc.vector.tensor_reduce(slot[:, k, :], picked[:, :, :], AX.X, ALU.add))
            link(nc.vector.tensor_copy(slot_i[:, :, :], slot[:, :, :]))
            nc.vector.tensor_scalar(tile_i[:, :, :], slot_i[:, :, :], 7, None, ALU.arith_shift_right)
            link(nc.vector.tensor_scalar(row_i[:, :, :], slot_i[:, :, :], P - 1, None, ALU.bitwise_and))
            link(nc.vector.tensor_copy(row_f[:, :, :], row_i[:, :, :]))
            for k in range(TOP_K):
                nc.vector.tensor_tensor(hot_tile[:, k, :, :],
                                        tile_i[:, k, :].unsqueeze(2).broadcast_to((P, T, RT)),
                                        iota_t[:, :].unsqueeze(1).broadcast_to((P, T, RT)), ALU.is_equal)
            for k in range(TOP_K):
                for t in range(T):
                    ins = nc.vector.tensor_scalar(hot_row[:, k, t, :], iota_p[:, :], row_f[:, k, t:t + 1],
                                                  token_id[:, t:t + 1], ALU.is_equal, ALU.mult)
                    if t % 8 == 7:
                        ins.then_inc(hot_ready, 1)
            nc.vector.tensor_scalar(fetch[:, :, :], slot[:, :, :], float(R * CAP - 1), None,
                                    ALU.min).then_inc(fetch_ready, 1)
            nc.vector.tensor_scalar(kept_routed[:, :, :], slot[:, :, :], float(R * CAP), None, ALU.is_lt)
            dve.wait_ge(gap_exp_ready, 1)
            link(nc.vector.tensor_scalar(gate_sum[:, :], gap_exp[:, :], 1.0, None, ALU.add))
            link(nc.vector.reciprocal(gate[0][:, :], gate_sum[:, :]))
            link(nc.vector.tensor_tensor(gate[1][:, :], gate[0][:, :], gap_exp[:, :], ALU.mult))
            for k in range(TOP_K):
                nc.vector.tensor_tensor(gate_routed[k][:, :], gate[k][:, :], kept_routed[:, k, :], ALU.mult)
            link(nc.vector.tensor_tensor(gate_dense[:, :, :], chosen[0][:, :, :], over_experts(gate[0][:, :]), ALU.mult))
            link(nc.vector.tensor_tensor(gate_part[:, :, :], chosen[1][:, :, :], over_experts(gate[1][:, :]), ALU.mult))
            link(nc.vector.tensor_tensor(gate_dense[:, :, :], gate_dense[:, :, :], gate_part[:, :, :], ALU.add))
            link(nc.vector.tensor_tensor(gate_dense[:, :, :], gate_dense[:, :, :], kept[:, :, :], ALU.mult))
            dve.wait_ge(slots_ready, 1)
            nc.vector.tensor_copy(slot_token[:, :], bank_y[1][:, 384:384 + RT]).then_inc(list_ready, 1)

            dve.wait_ge(std2_ready, 1)
            nc.vector.reciprocal(inv2[:, :], std2[:, :]).then_inc(dve_step, 1)
            count[0] += 1
            dve.wait_ge(dve_step, count[0])
            dve.wait_ge(bias_ready, 1)
            for t in range(T + 1):
                if t < T:
                    dve.wait_ge(qkv_raw, t + 1)
                    if t >= 3:
                        dve.wait_ge(kv_added, t - 2)
                    nc.vector.scalar_tensor_tensor(pre[t % 3][:, 0:QKV], bank_h[t % 4][:, 0:QKV], inv2[:, t:t + 1],
                                                   bias[:, :], ALU.mult, ALU.add).then_inc(pre_ready, 1)
                if t >= 1:
                    u = t - 1
                    dve.wait_ge(exp_ready, u + 1)
                    link(nc.vector.tensor_scalar(expo[u % 2][:, :], expo[u % 2][:, :], 1.0, None, ALU.min))
                    if u >= 2:
                        dve.wait_ge(kv_added, u - 1)
                    nc.vector.scalar_tensor_tensor(qk[u % 2][:, :], pre[u % 3][:, 0:2 * D], 0.0, expo[u % 2][:, :],
                                                   ALU.max, ALU.add).then_inc(qk_ready, 1)
                if t >= TB and t % TB == 0:
                    b = t // TB - 1
                    dve.wait_ge(kv_added, t)
                    nc.vector.tensor_tensor(state[b][:, 0:D], bank_y[b][:, 0:D], head_block[:, :], ALU.mult)
                    nc.vector.tensor_scalar(state[b][:, D:KVW], head_cols[:, :], bank_y[b][:, D:D + 1], None,
                                            ALU.mult).then_inc(state_ready, 1)
            dve.wait_ge(acc_ready, G)
            for u in range(T // 2 + 1):
                if u < T // 2:
                    dve.wait_ge(att_raw, u + 1)
                    both = bank_h[u % 2][:, 0:2 * KVW].rearrange("p (t c) -> p t c", t=2)
                    link(nc.vector.tensor_scalar(den[:, :, :], both[:, :, D:KVW], DENOM_EPS, None, ALU.add))
                    link(nc.vector.reciprocal(den_inv[:, :, :], den[:, :, :]))
                    if u >= 2:
                        dve.wait_ge(attT_raw, u - 1)
                    for i in range(2):
                        ins = nc.vector.tensor_tensor(
                            att[u % 2][:, i, :].rearrange("p (h c) -> p h c", h=HEADS),
                            both[:, i, 0:D].rearrange("p (h c) -> p h c", h=HEADS),
                            den_inv[:, i, :].unsqueeze(2).broadcast_to((P, HEADS, HD)), ALU.mult)
                    ins.then_inc(att_ready, 1)
                if u >= 1:
                    v = u - 1
                    dve.wait_ge(proj_raw, v + 1)
                    nc.vector.tensor_tensor(acc[:, 2 * v:2 * v + 2, :], acc[:, 2 * v:2 * v + 2, :],
                                            bank_h[2 + v % 2][:, 0:2 * D].rearrange("p (t d) -> p t d", t=2),
                                            ALU.add).then_inc(proj_added, 1)

            def split_gathered(s):
                r = steps[s][3]
                cols = steps[s][2] * P
                dve.wait_ge(xg_hi_ready, r + 1)
                nc.vector.tensor_tensor(xg_lo[r % 2][:, 0:cols], bank_x[r % 2][:, 0:cols],
                                        xg_hi[r % 2][:, 0:cols].bitcast(F32),
                                        ALU.subtract).then_inc(xg_lo_ready, 1)

            def add_dense(s):
                e, t0, nt, r = steps[s]
                if r is not None:
                    return
                dve.wait_ge(down_done, s + 1)
                if s > dense_steps[0]:
                    dve.wait_ge(y_added, dense_steps.index(s))
                for j in range(nt):
                    ins = nc.vector.scalar_tensor_tensor(
                        acc[:, t0 + j, :], bank_y[s % 2][:, j * D:(j + 1) * D], gate_dense[:, t0 + j, e:e + 1],
                        acc[:, t0 + j, :], ALU.mult, ALU.add)
                ins.then_inc(y_added, 1)

            dve.wait_ge(proj_added, T // 2)
            if steps[0][3] is not None:
                split_gathered(0)
            for s in range(S):
                cols = steps[s][2] * P
                for c in range(FC):
                    i = FC * s + c
                    dve.wait_ge(gelu_ready, i + 1)
                    if c == 0 and s >= 2:
                        dve.wait_ge(down_done, s - 1)
                    nc.vector.tensor_tensor(hid[s % 2][:, c, 0:cols], gelu[i % 2][:, 0:cols],
                                            bank_h[2 * c + 1][:, 0:cols], ALU.mult).then_inc(hid_ready, 1)
                if s + 1 < S and steps[s + 1][3] is not None:
                    split_gathered(s + 1)
                if s >= 1:
                    add_dense(s - 1)
            add_dense(S - 1)

            if dense_steps:
                dve.wait_ge(y_added, len(dense_steps))
            for n in range(T * TOP_K):
                t, k = n // TOP_K, n % TOP_K
                dve.wait_ge(fetched_in[n % CR], 16 * (n // CR + 1))
                if k > 0:
                    dve.wait_ge(fetched_used, n)
                nc.vector.scalar_tensor_tensor(acc[:, t, :], fetched[n % CR][:, :], gate_routed[k][:, t:t + 1],
                                               acc[:, t, :], ALU.mult, ALU.add).then_inc(fetched_used, 1)

        @block.tensor
        def _(pe):
            def product(dst, halves, last=None):
                (a_hi, a_lo), (b_hi, b_lo) = halves
                nc.tensor.matmul(dst, a_lo, b_hi, start=True, stop=False)
                nc.tensor.matmul(dst, a_hi, b_lo, start=False, stop=False)
                return nc.tensor.matmul(dst, a_hi, b_hi, start=False, stop=True)

            def x_halves(t):
                return xT_hi[:, t * P:(t + 1) * P], xT_lo[:, t * P:(t + 1) * P]

            def transpose_group(g):
                pe.wait_ge(xn_ready, g + 1)
                if g >= 2:
                    pe.wait_ge(xT_lo_ready, g - 1)
                for j in range(GROUP):
                    ins = nc.tensor.transpose(bank_x[g % 2][:, j * P:(j + 1) * P], xn[:, g * GROUP + j, :],
                                              ident[:, :])
                ins.then_inc(xT_raw, 1)

            def logits_group(g):
                pe.wait_ge(xT_lo_ready, g + 1)
                for t in range(g * GROUP, (g + 1) * GROUP):
                    ins = product(bank_y[0][:, t * E:(t + 1) * E], (x_halves(t), (wg_hi[:, :], wg_lo[:, :])))
                if g == G - 1:
                    ins.then_inc(logits_ready, 1)

            pe.wait_ge(const_ready, 1)
            transpose_group(0)
            pe.wait_ge(wsmall_ready, 1)
            for g in range(1, G):
                transpose_group(g)
                logits_group(g - 1)
            logits_group(G - 1)
            nc.tensor.matmul(bank_y[1][:, 0:QKV], beta_cols[:, :], wqkv_sb[:, :],
                             start=True, stop=True).then_inc(bias_raw, 1)

            def qkv_tile(t):
                if t >= 4:
                    pe.wait_ge(pre_ready, t - 3)
                product(bank_h[t % 4][:, 0:QKV], (x_halves(t), (wqkv_hi[:, :], wqkv_lo[:, :]))).then_inc(qkv_raw, 1)

            for t in range(4):
                qkv_tile(t)
            pe.wait_ge(assigned_ready, 1)
            before = bank_y[0][:, 128:128 + T * E]
            nc.tensor.matmul(before, earlier[:, :], assigned[:, :, :], start=True, stop=False)
            for t in range(T - 1):
                ins = nc.tensor.matmul(before[:, (t + 1) * E:].rearrange("p (t e) -> p t e", e=E), ones_bf[:, :],
                                       assigned[:, t:t + 1, :].broadcast_to((P, T - 1 - t, E)),
                                       start=False, stop=(t == T - 2))
            ins.then_inc(before_ready, 1)
            pe.wait_ge(bias_ready, 1)
            for n in range(TOP_K * T):
                k, t = n // T, n % T
                if t % 8 == 0:
                    pe.wait_ge(hot_ready, n // 8 + 1)
                ins = nc.tensor.matmul(bank_y[1][:, 384:384 + RT], hot_row[:, k, t, :], hot_tile[:, k, t, :],
                                       start=(n == 0), stop=(n == TOP_K * T - 1))
            ins.then_inc(slots_ready, 1)

            def transpose_queries(t):
                if t % GROUP == 0 and t >= 2 * GROUP:
                    pe.wait_ge(qT_ready, t // GROUP - 1)
                return nc.tensor.transpose(bank_x[(t // GROUP) % 2][:, (t % GROUP) * P:(t % GROUP + 1) * P],
                                           qk[t % 2][:, 0:D], ident[:, :])

            for t in range(T):
                if t + 4 < T:
                    qkv_tile(t + 4) if t >= 0 else None
                pe.wait_ge(qk_ready, t + 1)
                if t == 0:
                    pe.wait_ge(list_ready, 1)
                ins = transpose_queries(t)
                if t % GROUP == GROUP - 1:
                    ins.then_inc(qT_raw, 1)
                b = t // TB
                nc.tensor.matmul(bank_y[b][:, 0:D + 2], qk[t % 2][:, D:2 * D], pre[t % 3][:, 2 * D:QKV + 2],
                                 start=(t % TB == 0), stop=(t % TB == TB - 1)).then_inc(kv_added, 1)

            def project(u):
                pe.wait_ge(attT_ready, u + 1)
                if u >= 2:
                    pe.wait_ge(proj_added, u - 1)
                for i in range(2):
                    ins = nc.tensor.matmul(bank_h[2 + u % 2][:, i * D:(i + 1) * D], attT[u % 2][:, i * P:(i + 1) * P],
                                           wout_sb[:, :], start=True, stop=True)
                ins.then_inc(proj_raw, 1)

            for u in range(T // 2 + 1):
                if u < T // 2:
                    b = 2 * u // TB
                    pe.wait_ge(state_ready, b + 1)
                    if u == 0:
                        pe.wait_ge(qT_ready, G)
                        pe.wait_ge(pre_ready, T)
                    if u >= 2:
                        pe.wait_ge(att_ready, u - 1)
                    for i in range(2):
                        t = 2 * u + i
                        ins = nc.tensor.matmul(bank_h[u % 2][:, i * KVW:(i + 1) * KVW], qT[:, t * P:(t + 1) * P],
                                               state[b][:, :], start=True, stop=True)
                    ins.then_inc(att_raw, 1)
                if u >= 1:
                    project(u - 1)
                if u < T // 2:
                    pe.wait_ge(att_ready, u + 1)
                    if u >= 2:
                        pe.wait_ge(attT_ready, u - 1)
                    for i in range(2):
                        ins = nc.tensor.transpose(bank_x[u % 2][:, i * P:(i + 1) * P], att[u % 2][:, i, :], ident[:, :])
                    ins.then_inc(attT_raw, 1)

            def transpose_slots(s):
                e, j0, nj, r = steps[s]
                if j0 == 0:
                    pe.wait_ge(rows_in[e - DENSE], 16 * ST)
                if r >= 2:
                    pe.wait_ge(xg_lo_ready, r - 1)
                for j in range(nj):
                    n = (e - DENSE) * ST + j0 + j
                    ins = nc.tensor.transpose(bank_x[r % 2][:, j * P:(j + 1) * P], gathered[:, n, :], ident[:, :])
                ins.then_inc(xg_raw, 1)

            def up(s):
                e, j0, nj, r = steps[s]
                cols = nj * P
                if r is None:
                    right = xT_hi[:, j0 * P:j0 * P + cols], xT_lo[:, j0 * P:j0 * P + cols]
                else:
                    pe.wait_ge(xg_lo_ready, r + 1)
                    right = xg_hi[r % 2][:, 0:cols], xg_lo[r % 2][:, 0:cols]
                pe.wait_ge(w1_lo_ready, order_of_experts.index(e) + 1)
                for c in range(FC):
                    if s >= 1:
                        pe.wait_ge(gelu_ready, FC * (s - 1) + c + 1)
                        pe.wait_ge(hid_ready, FC * (s - 1) + c + 1)
                    for i, first in enumerate((c * P, F + c * P)):
                        left = w1_hi[:, e, first:first + P], w1_lo[:, e, first:first + P]
                        ins = product(bank_h[2 * c + i][:, 0:cols], (left, right))
                    ins.then_inc(up_done, 1)

            def down(s):
                e, _, nj, _ = steps[s]
                pe.wait_ge(hid_ready, FC * (s + 1))
                y_freed(pe, s)
                if s == 0:
                    pe.wait_ge(w_in[e], 32)
                for j in range(nj):
                    for c in range(FC):
                        ins = nc.tensor.matmul(bank_y[s % 2][:, j * D:(j + 1) * D], hid[s % 2][:, c, j * P:(j + 1) * P],
                                               w2_sb[:, e, c, :], start=(c == 0), stop=(c == FC - 1))
                ins.then_inc(down_done, 1)

            pe.wait_ge(proj_added, T // 2)
            pe.wait_ge(attT_ready, T // 2)
            if steps[0][3] is not None:
                transpose_slots(0)
            for s in range(S):
                up(s)
                if s + 1 < S and steps[s + 1][3] is not None:
                    transpose_slots(s + 1)
                if s >= 1:
                    down(s - 1)
            down(S - 1)


def kernel(L0_attn_x, L0_attn_gamma, L0_attn_beta, L0_attn_Wqkv, L0_attn_Wout, L0_ffn_Wg, L0_ffn_W1, L0_ffn_W2):
    import numpy as np
    import concourse.bacc as bacc
    from concourse.bass_utils import run_bass_kernel_spmd

    laid_out = {
        "x": L0_attn_x,
        "gamma": np.asarray(L0_attn_gamma).reshape(-1, 1),
        "beta": np.asarray(L0_attn_beta).reshape(-1, 1),
        "wqkv": L0_attn_Wqkv,
        "wout": L0_attn_Wout,
        "wg_t": np.asarray(L0_ffn_Wg).T,
        "w1": L0_ffn_W1,
        "w2": L0_ffn_W2,
    }
    nc = bacc.Bacc("TRN2", target_bir_lowering=False, num_devices=1)
    arrays, args = {}, []
    for name, a in laid_out.items():
        a = np.ascontiguousarray(a)
        arrays[f"in_{name}"] = a
        args.append(nc.dram_tensor(f"in_{name}", a.shape, mybir.dt.from_np(a.dtype), kind="ExternalInput").ap())
    shape = np.asarray(L0_attn_x).shape
    args.append(nc.dram_tensor("out_block", shape, F32, kind="ExternalOutput").ap())
    moe_attention_block(nc, *args)
    r = run_bass_kernel_spmd(nc, [arrays], core_ids=[0])
    return r.results[0]["out_block"]
```

```python
from contextlib import ExitStack

import concourse.bass as bass
from concourse import mybir

F32 = mybir.dt.float32
F32R = mybir.dt.float32r
F16 = mybir.dt.float16
BF16 = mybir.dt.bfloat16
I32 = mybir.dt.int32
ALU = mybir.AluOpType
ACT = mybir.ActivationFunctionType
AX = mybir.AxisListType

P = 128
LN_EPS = 1e-5
DENOM_EPS = 1e-6
HEADS = 16
TOP_K = 2
CAPACITY_FACTOR = 1.25
GROUP = 4
DENSE = 1
DENSE_FIRST = 0
ATT_FROM = 12
ATT_PIECES = 1
FETCHED_FROM = 17
FETCHED_PIECES = 4
W1_EARLY = 2
LO_EARLY = 2
PRE_POOL = 6
DROPPED = 8192.0
PARTS = ((0, 3), (3, 2))


def moe_attention_block(nc, x, gamma, beta, wqkv, wout, wg_t, w1, w2, out):
    B, L, D = x.shape
    N = B * L
    E, _, F2 = w1.shape
    F = F2 // 2
    T = N // P
    G = T // GROUP
    TB = L // P
    CAP = int(N * TOP_K * CAPACITY_FACTOR / E)
    ST = CAP // P
    R = E - DENSE
    RT = R * ST
    HD = D // HEADS
    FC = F // P
    QKV = 3 * D
    KVW = D + HEADS
    assert D == P and CAP % P == 0 and sum(n for _, n in PARTS) == ST and N <= 2048 and FC == 2

    routed_steps = [(e, j0, nj) for e in range(DENSE, E) for j0, nj in PARTS]
    all_token_steps = [(e, g * GROUP, GROUP, None) for e in range(DENSE) for g in range(G)]
    steps = all_token_steps[:DENSE_FIRST]
    steps += [(e, j0, nj, r) for r, (e, j0, nj) in enumerate(routed_steps)]
    steps += all_token_steps[DENSE_FIRST:]
    S = len(steps)
    step_of_routed = [s for s in range(S) if steps[s][3] is not None]
    dense_steps = [s for s in range(S) if steps[s][3] is None]
    U = T // 2
    KT = TOP_K * T
    pieces = [[("numerators", 0)]]
    for u in range(U):
        pieces.append([("transposes", u)])
        pieces.append([("projection", u)] + ([("numerators", u + 1)] if u + 1 < U else []))
    chunks = [(s, c) for s in range(S) for c in range(FC)]
    pieces_at = {}
    for i, piece in enumerate(pieces):
        i = FC * ATT_FROM + i // ATT_PIECES
        pieces_at.setdefault(chunks[i] if i < len(chunks) else "end", []).extend(piece)
    fetched_at = {}
    for n in range(KT):
        i = FC * FETCHED_FROM + n // FETCHED_PIECES
        fetched_at.setdefault(chunks[i] if i < len(chunks) else "end", []).append(n)

    sum_tiles, sums_with = [], {}

    def note_sum(name, tiles):
        sum_tiles.append(tiles)
        sums_with[name] = len(sum_tiles)

    for s, c in chunks + [(S, 0)]:
        for kind, u in pieces_at.get((s, c), []):
            if kind == "projection":
                note_sum((kind, u), (2 * u, 2 * u + 1))
        for n in fetched_at.get((s, c), []):
            note_sum(("fetched", n), (n // TOP_K,))
        if s >= 1 and (c == FC - 1 or s == S) and steps[s - 1][3] is None:
            for j in range(GROUP):
                note_sum(("step", s - 1), (steps[s - 1][1] + j,))
    for kind, u in pieces_at.get("end", []):
        if kind == "projection":
            note_sum((kind, u), (2 * u, 2 * u + 1))
    for n in fetched_at.get("end", []):
        note_sum(("fetched", n), (n // TOP_K,))

    def earlier_sum(index, tiles):
        return max([i + 1 for i in range(index) if set(sum_tiles[i]) & set(tiles)], default=0)

    x_tiles = x.rearrange("b (t p) d -> p (b t) d", p=P)
    out_tiles = out.rearrange("b (t p) d -> p (b t) d", p=P)
    xn_rows = nc.dram_tensor("xn_rows", [N, D], F32).ap()
    y_rows = nc.dram_tensor("y_rows", [R * CAP, D], F32).ap()
    xn_rows_tiles = xn_rows.rearrange("(t p) d -> p t d", p=P)
    y_rows_tiles = y_rows.rearrange("(t p) d -> p t d", p=P)

    with ExitStack() as ctx:
        def sb(name, shape, dt=F32):
            return ctx.enter_context(nc.sbuf_tensor(name, shape, dt))

        def sem(name):
            return ctx.enter_context(nc.semaphore(name))

        xs = sb("xs", [P, T, D])
        acc = xs
        xn = sb("xn", [P, T, D])
        xT_hi = sb("xT_hi", [P, N], F32R)
        xT_lo = sb("xT_lo", [P, N], F32R)
        w1_raw = sb("w1_raw", [P, E, F2])
        w1_hi = sb("w1_hi", [P, E, F2], F32R)
        w1_lo = sb("w1_lo", [P, E, F2], F32R)
        w2_sb = sb("w2_sb", [P, E, FC, D])
        wqkv_sb = sb("wqkv_sb", [P, QKV])
        wqkv_hi = sb("wqkv_hi", [P, QKV], F32R)
        wqkv_lo = sb("wqkv_lo", [P, QKV], F32R)
        wout_sb = sb("wout_sb", [P, D])
        wg_sb = sb("wg_sb", [P, E])
        gamma_sb = sb("gamma_sb", [P, 1])
        beta_sb = sb("beta_sb", [P, 1])
        bias = sb("bias", [P, QKV])

        ident = sb("ident", [P, P])
        earlier = sb("earlier", [P, P], BF16)
        ones_bf = sb("ones_bf", [P, P], BF16)
        head_block = sb("head_block", [P, D])
        head_cols = sb("head_cols", [P, HEADS])
        iota_tiles = sb("iota_tiles", [P, RT, KT], F16)
        token_id = sb("token_id", [P, TOP_K, T], F16)
        first_slot = sb("first_slot", [P, T, E])
        rank = sb("rank", [P, T, E])
        eps = sb("eps", [P, 1])
        unused = sb("unused", [P, 1])
        unused_gelu = sb("unused_gelu", [P, 1])

        stats = sb("stats", [P, T, 6])
        mv = sb("mv", [P, T, 2])
        std1 = sb("std1", [P, T])
        inv1 = sb("inv1", [P, T])
        nmi = sb("nmi", [P, T])
        var2 = sb("var2", [P, T])
        std2 = sb("std2", [P, T])
        inv2 = sb("inv2", [P, T])

        logit = sb("logit", [P, T, E])
        rest = sb("rest", [P, T, E])
        eq = sb("eq", [P, T, E])
        chosen = sb("chosen", [P, TOP_K, T, E])
        top = [sb(f"top{k}", [P, T]) for k in range(TOP_K)]
        best = sb("best", [P, T])
        gap = sb("gap", [P, T])
        gap_exp = sb("gap_exp", [P, T])
        gate_sum = sb("gate_sum", [P, T])
        gate = [sb(f"gate{k}", [P, T]) for k in range(TOP_K)]
        gate_routed = [sb(f"gate_routed{k}", [P, T]) for k in range(TOP_K)]
        assigned = sb("assigned", [P, T, E], BF16)
        kept = sb("kept", [P, T, E])
        slot_all = sb("slot_all", [P, T, E])
        drop = sb("drop", [P, T, E])
        picked = sb("picked", [P, TOP_K, T, E])
        slot = sb("slot", [P, TOP_K, T])
        slot_i = sb("slot_i", [P, TOP_K, T], I32)
        row_i = sb("row_i", [P, TOP_K, T], I32)
        tile_i = sb("tile_i", [P, TOP_K, T], I32)
        row_16 = sb("row_16", [P, TOP_K, T], F16)
        tile_16 = sb("tile_16", [P, TOP_K, T], F16)
        kept_routed = sb("kept_routed", [P, TOP_K, T])
        fetch = sb("fetch", [P, TOP_K, T], I32)
        gate_dense = sb("gate_dense", [P, T, E])
        gate_part = sb("gate_part", [P, T, E])
        hot_tile = sb("hot_tile", [P, RT, KT], F16)
        hot_token = sb("hot_token", [P, RT, KT], F16)
        slot_token = sb("slot_token", [P, RT], I32)

        gathered = sb("gathered", [P, RT, D])
        iota_rows = gathered[:, :, :].rearrange("p n d -> p (n d)")[:, 0:P * KT // 2] \
            .bitcast(F16).rearrange("p (r n) -> p r n", n=KT)
        xg_hi = [sb(f"xg_hi{i}", [P, 3 * P], F32R) for i in range(2)]
        xg_lo = [sb(f"xg_lo{i}", [P, 3 * P], F32R) for i in range(2)]
        gelu = [sb(f"gelu{i}", [P, GROUP * P]) for i in range(2)]
        wqkv_g, beta_cols = gelu[0][:, 0:QKV], gelu[1][:, 0:P]
        hid = [sb(f"hid{i}", [P, FC, GROUP * P]) for i in range(2)]
        y_sb = [sb(f"y_sb{i}", [P, 3, D]) for i in range(2)]

        pre = sb("pre", [P, T, 2 * D])
        xT = pre[:, T // 2:T, :].rearrange("p t n -> p (t n)")
        val = sb("val", [P, T, D + 2])
        expo = sb("expo", [P, T, 2 * D])
        qT = sb("qT", [P, N])
        hot_row = qT[:, 0:P * KT // 2].bitcast(F16).rearrange("p (r n) -> p r n", n=KT)
        state = [sb(f"state{b}", [P, KVW]) for b in range(B)]
        den = sb("den", [P, 2, HEADS])
        den_inv = sb("den_inv", [P, 2, HEADS])
        att = [sb(f"att{i}", [P, 2, D]) for i in range(2)]
        v_bias = [att[b][:, 0, :] for b in range(B)]
        attT = [sb(f"attT{i}", [P, 2 * P]) for i in range(2)]
        fetched = expo[:, :, :].rearrange("p t (k d) -> p (t k) d", k=TOP_K)

        bank_x = [ctx.enter_context(nc.psum_tensor(f"bank_x{i}", [P, 512], F32)) for i in range(2)]
        bank_h = [ctx.enter_context(nc.psum_tensor(f"bank_h{i}", [P, 512], F32)) for i in range(4)]
        bank_y = ctx.enter_context(nc.psum_tensor("bank_y", [P, 512], F32))
        bank_a = ctx.enter_context(nc.psum_tensor("bank_a", [P, 512], F32))

        x_in = [sem(f"x_in{g}") for g in range(G)]
        small_in = sem("small_in")
        w1_in = [sem(f"w1_in{i}") for i in range(E // 2)]
        w2_in = [sem(f"w2_in{i}") for i in range(2)]
        xn_stored = sem("xn_stored")
        rows_in = [sem(f"rows_in{e}") for e in range(R)]
        y_stored = [sem(f"y_stored{i}") for i in range(2)]
        fetched_in = [sem(f"fetched_in{g}") for g in range(2 * G)]
        out_stored = sem("out_stored")
        ident_ready = sem("ident_ready")
        const_ready = sem("const_ready")
        pool_step = sem("pool_step")
        dve_step = sem("dve_step")
        eps_ready = sem("eps_ready")
        mv_ready = sem("mv_ready")
        std1_ready = sem("std1_ready")
        nmi_ready = sem("nmi_ready")
        xn_ready = sem("xn_ready")
        xn_act_ready = sem("xn_act_ready")
        xT_raw = sem("xT_raw")
        xT_hi_ready = sem("xT_hi_ready")
        xT_lo_ready = sem("xT_lo_ready")
        xT_late_ready = sem("xT_late_ready")
        xT_ready = sem("xT_ready")
        wsmall_ready = sem("wsmall_ready")
        logits_ready = sem("logits_ready")
        acc_ready = sem("acc_ready")
        w1_hi_ready = sem("w1_hi_ready")
        w1_lo_ready = sem("w1_lo_ready")
        w1_late_ready = sem("w1_late_ready")
        gap_ready = sem("gap_ready")
        gap_exp_ready = sem("gap_exp_ready")
        assigned_ready = sem("assigned_ready")
        before_ready = sem("before_ready")
        hot_ready = sem("hot_ready")
        slots_ready = sem("slots_ready")
        list_ready = sem("list_ready")
        fetch_ready = sem("fetch_ready")
        gates_ready = sem("gates_ready")
        ones_ready = sem("ones_ready")
        bias_raw = sem("bias_raw")
        bias_ready = sem("bias_ready")
        var2_ready = sem("var2_ready")
        std2_ready = sem("std2_ready")
        qkv_raw = sem("qkv_raw")
        scaled_ready = sem("scaled_ready")
        pre_ready = sem("pre_ready")
        pre_late_ready = sem("pre_late_ready")
        val_ready = sem("val_ready")
        exp_ready = sem("exp_ready")
        qk_ready = sem("qk_ready")
        kv_added = sem("kv_added")
        qT_raw = sem("qT_raw")
        qT_ready = sem("qT_ready")
        state_ready = sem("state_ready")
        att_raw = sem("att_raw")
        att_ready = sem("att_ready")
        attT_raw = sem("attT_raw")
        attT_ready = sem("attT_ready")
        proj_raw = sem("proj_raw")
        xg_raw = sem("xg_raw")
        xg_hi_ready = sem("xg_hi_ready")
        xg_lo_ready = sem("xg_lo_ready")
        up_done = sem("up_done")
        gelu_ready = sem("gelu_ready")
        hid_ready = sem("hid_ready")
        down_done = sem("down_done")
        y_evac = sem("y_evac")
        acc_added = sem("acc_added")

        block = ctx.enter_context(nc.Block())

        @block.sync
        def _(sp):
            for g in range(G):
                sp.dma_start(xs[:, g * GROUP:(g + 1) * GROUP, :],
                             x_tiles[:, g * GROUP:(g + 1) * GROUP, :]).then_inc(x_in[g], 16)
            for i in range(E // 2):
                sp.dma_start(w1_raw[:, 2 * i:2 * i + 2, :],
                             w1[2 * i:2 * i + 2].rearrange("e p n -> p e n")).then_inc(w1_in[i], 16)
                if i == 0:
                    sp.dma_start(w2_sb[:, 0:2, :, :],
                                 w2[0:2].rearrange("e (c p) d -> p e c d", p=P)).then_inc(w2_in[0], 16)
            sp.dma_start(w2_sb[:, 2:E, :, :],
                         w2[2:E].rearrange("e (c p) d -> p e c d", p=P)).then_inc(w2_in[1], 16)
            for g in range(G):
                sp.wait_ge(xn_ready, g + 1)
                sp.wait_ge(xn_act_ready, g + 1)
                sp.dma_start(xn_rows_tiles[:, g * GROUP:(g + 1) * GROUP, :],
                             xn[:, g * GROUP:(g + 1) * GROUP, :]).then_inc(xn_stored, 16)
            for r, (e, j0, nj) in enumerate(routed_steps):
                sp.wait_ge(y_evac, r + 1)
                t0 = (e - DENSE) * ST + j0
                sp.dma_start(y_rows_tiles[:, t0:t0 + nj, :],
                             y_sb[r % 2][:, 0:nj, :]).then_inc(y_stored[r % 2], 16)
            for g in range(G):
                sp.wait_ge(acc_added, earlier_sum(len(sum_tiles), range(g * GROUP, (g + 1) * GROUP)))
                sp.dma_start(out_tiles[:, g * GROUP:(g + 1) * GROUP, :],
                             acc[:, g * GROUP:(g + 1) * GROUP, :]).then_inc(out_stored, 16)
            sp.wait_ge(out_stored, 16 * G)

        @block.gpsimd
        def _(pool):
            count = [0]

            def link(ins):
                count[0] += 1
                ins.then_inc(pool_step, 1)
                pool.wait_ge(pool_step, count[0])

            link(nc.gpsimd.memset(ident[:], 0.0))
            nc.gpsimd.affine_select(out=ident[:], in_=ident[:], compare_op=ALU.not_equal, fill=1.0,
                                    base=0, pattern=[[-1, P]], channel_multiplier=1).then_inc(ident_ready, 1)
            link(nc.gpsimd.memset(earlier[:], 1.0))
            nc.gpsimd.affine_select(out=earlier[:], in_=earlier[:], compare_op=ALU.is_gt, fill=0.0,
                                    base=0, pattern=[[1, P]], channel_multiplier=-1)
            nc.gpsimd.memset(ones_bf[:], 1.0)
            link(nc.gpsimd.memset(head_cols[:], 1.0))
            link(nc.gpsimd.affine_select(out=head_cols[:], in_=head_cols[:], compare_op=ALU.is_ge, fill=0.0,
                                         base=0, pattern=[[-HD, HEADS]], channel_multiplier=1))
            link(nc.gpsimd.affine_select(out=head_cols[:], in_=head_cols[:], compare_op=ALU.is_ge, fill=0.0,
                                         base=HD - 1, pattern=[[HD, HEADS]], channel_multiplier=-1))
            nc.gpsimd.tensor_copy(head_block[:, :].rearrange("p (h c) -> p h c", h=HEADS),
                                  head_cols[:, :].unsqueeze(2).broadcast_to((P, HEADS, HD)))
            nc.gpsimd.iota(token_id[:], pattern=[[0, TOP_K], [P, T]], base=0, channel_multiplier=1,
                           allow_small_or_imprecise_dtypes=True)
            nc.gpsimd.iota(rank[:], pattern=[[0, T], [-1, E]], base=E, channel_multiplier=0,
                           allow_small_or_imprecise_dtypes=True)
            link(nc.gpsimd.memset(first_slot[:], DROPPED))
            nc.gpsimd.iota(iota_tiles[:], pattern=[[1, RT], [0, KT]], base=0, channel_multiplier=0,
                           allow_small_or_imprecise_dtypes=True)
            nc.gpsimd.iota(iota_rows[:, :, :], pattern=[[1, P], [0, KT]], base=0, channel_multiplier=0,
                           allow_small_or_imprecise_dtypes=True)
            nc.gpsimd.iota(first_slot[:, :, DENSE:E], pattern=[[0, T], [CAP, R]], base=0,
                           channel_multiplier=0, allow_small_or_imprecise_dtypes=True).then_inc(const_ready, 1)

            def lower_w1(e):
                pool.wait_ge(w1_hi_ready, e + 1)
                nc.gpsimd.tensor_tensor(w1_lo[:, e, :], w1_raw[:, e, :], w1_hi[:, e, :].bitcast(F32),
                                        ALU.subtract).then_inc(w1_lo_ready, 1)

            for g in range(LO_EARLY):
                pool.wait_ge(xT_hi_ready, g + 1)
                nc.gpsimd.tensor_tensor(xT_lo[:, g * 512:(g + 1) * 512], xT[:, g * 512:(g + 1) * 512],
                                        xT_hi[:, g * 512:(g + 1) * 512].bitcast(F32),
                                        ALU.subtract).then_inc(xT_lo_ready, 1)
            for e in range(W1_EARLY):
                lower_w1(e)
            pool.wait_ge(bias_ready, 1)
            for t in range(PRE_POOL):
                pool.wait_ge(scaled_ready, t + 1)
                nc.gpsimd.tensor_tensor(pre[:, t, :], pre[:, t, :], bias[:, 0:2 * D],
                                        ALU.add).then_inc(pre_ready, 1)
            pool.wait_ge(xn_stored, 16 * G)
            pool.wait_ge(list_ready, 1)
            for n in range(RT):
                nc.gpsimd.indirect_dma_start(
                    gathered[:, n, :], None, xn_rows,
                    bass.IndirectOffsetOnAxis(ap=slot_token[:, n:n + 1], axis=0),
                ).then_inc(rows_in[n // ST], 16)
            for i in range(2):
                pool.wait_ge(y_stored[i], 16 * len(range(i, len(routed_steps), 2)))
            pool.wait_ge(fetch_ready, 1)
            for n in range(T * TOP_K):
                t, k = n // TOP_K, n % TOP_K
                nc.gpsimd.indirect_dma_start(
                    fetched[:, n, :], None, y_rows,
                    bass.IndirectOffsetOnAxis(ap=fetch[:, k, t:t + 1], axis=0),
                ).then_inc(fetched_in[n // 4], 16)

        @block.scalar
        def _(act):
            act.dma_start(wqkv_sb[:, :], wqkv).then_inc(small_in, 16)
            act.dma_start(wg_sb[:, :], wg_t).then_inc(small_in, 16)
            act.dma_start(gamma_sb[:, :], gamma).then_inc(small_in, 16)
            act.dma_start(beta_sb[:, :], beta).then_inc(small_in, 16)
            act.dma_start(wout_sb[:, :], wout).then_inc(small_in, 16)
            def root(g):
                act.wait_ge(mv_ready, g + 1)
                nc.scalar.activation(std1[:, g * GROUP:(g + 1) * GROUP], mv[:, g * GROUP:(g + 1) * GROUP, 1],
                                     ACT.Sqrt, bias=eps[:, 0:1]).then_inc(std1_ready, 1)

            def normalise(g):
                act.wait_ge(nmi_ready, g + 1)
                for t in range(g * GROUP + 2, (g + 1) * GROUP):
                    ins = nc.scalar.activation(xn[:, t, :], xs[:, t, :], ACT.Identity, scale=inv1[:, t:t + 1],
                                               bias=nmi[:, t:t + 1])
                ins.then_inc(xn_act_ready, 1)

            def transposed(g):
                act.wait_ge(xT_raw, g + 1)
                nc.scalar.activation(xT[:, g * 512:(g + 1) * 512], bank_x[g % 2][:, :],
                                     ACT.Copy).then_inc(xT_ready, 1)

            def upper_transposed(g):
                act.wait_ge(xT_ready, g + 1)
                nc.scalar.activation(xT_hi[:, g * 512:(g + 1) * 512], xT[:, g * 512:(g + 1) * 512],
                                     ACT.Copy).then_inc(xT_hi_ready, 1)

            def upper_w1(i):
                act.wait_ge(w1_in[i], 16)
                for e in (2 * i, 2 * i + 1):
                    nc.scalar.activation(w1_hi[:, e, :], w1_raw[:, e, :], ACT.Copy).then_inc(w1_hi_ready, 1)

            act.wait_ge(eps_ready, 1)
            root(0)
            root(1)
            normalise(0)
            root(2)
            normalise(1)
            transposed(0)
            root(3)
            normalise(2)
            transposed(1)
            normalise(3)
            transposed(2)
            act.wait_ge(var2_ready, 1)
            nc.scalar.activation(std2[:, :], var2[:, :], ACT.Sqrt, bias=eps[:, 0:1]).then_inc(std2_ready, 1)
            upper_transposed(0)
            transposed(3)
            for g in range(1, G):
                upper_transposed(g)
            upper_w1(0)
            act.wait_ge(bias_raw, 1)
            nc.scalar.activation(bias[:, :], bank_a[:, 0:QKV], ACT.Copy).then_inc(bias_ready, 1)
            act.wait_ge(ones_ready, 1)

            def scaled_values(t):
                nc.scalar.activation(val[:, t, 0:D], bank_h[t % 4][:, 2 * D:QKV], ACT.Copy,
                                     scale=inv2[:, t:t + 1]).then_inc(val_ready, 1)

            for t in range(PRE_POOL):
                act.wait_ge(qkv_raw, t + 1)
                nc.scalar.activation(pre[:, t, :], bank_h[t % 4][:, 0:2 * D], ACT.Copy,
                                     scale=inv2[:, t:t + 1]).then_inc(scaled_ready, 1)
                scaled_values(t)
            nc.scalar.activation(unused[:, :], eps[:, :], ACT.Exp)
            for u in range(U):
                if 2 * u < PRE_POOL:
                    act.wait_ge(pre_ready, 2 * u + 2)
                else:
                    act.wait_ge(pre_late_ready, 2 * u + 2 - PRE_POOL)
                nc.scalar.activation(expo[:, 2 * u:2 * u + 2, :], pre[:, 2 * u:2 * u + 2, :], ACT.Exp)
                nc.scalar.activation(pre[:, 2 * u:2 * u + 2, :], pre[:, 2 * u:2 * u + 2, :],
                                     ACT.Relu).then_inc(exp_ready, 1)
                if 2 * u >= PRE_POOL:
                    scaled_values(2 * u)
                    scaled_values(2 * u + 1)
                if u == 1:
                    act.wait_ge(gap_ready, 1)
                    nc.scalar.activation(gap_exp[:, :], gap[:, :], ACT.Exp).then_inc(gap_exp_ready, 1)
            nc.scalar.activation(unused_gelu[:, :], eps[:, :], ACT.Gelu)
            for g in range(G):
                act.wait_ge(qT_raw, g + 1)
                nc.scalar.activation(qT[:, g * 512:(g + 1) * 512], bank_x[g % 2][:, :],
                                     ACT.Copy).then_inc(qT_ready, 1)

            def attention_piece(kind, u):
                if kind == "transposes":
                    act.wait_ge(attT_raw, u + 1)
                    if u >= 2:
                        act.wait_ge(proj_raw, u - 1)
                    nc.scalar.activation(attT[u % 2][:, :], bank_x[1][:, 0:2 * P],
                                         ACT.Copy).then_inc(attT_ready, 1)

            def split_gathered(s):
                r = steps[s][3]
                cols = steps[s][2] * P
                act.wait_ge(xg_raw, r + 1)
                if r >= 2:
                    act.wait_ge(up_done, FC * (step_of_routed[r - 2] + 1))
                nc.scalar.activation(xg_hi[r % 2][:, 0:cols], bank_x[0][:, 0:cols],
                                     ACT.Copy).then_inc(xg_hi_ready, 1)

            def evacuate(s):
                r = steps[s][3]
                if r is None:
                    return
                nj = steps[s][2]
                act.wait_ge(down_done, s + 1)
                if r >= 2:
                    act.wait_ge(y_stored[r % 2], 16 * (r // 2))
                nc.scalar.activation(y_sb[r % 2][:, 0:nj, :],
                                     bank_y[:, 0:nj * P].rearrange("p (j d) -> p j d", d=D),
                                     ACT.Copy).then_inc(y_evac, 1)

            if steps[0][3] is not None:
                split_gathered(0)
            for s in range(S):
                cols = steps[s][2] * P
                for c in range(FC):
                    i = FC * s + c
                    act.wait_ge(up_done, i + 1)
                    if i >= 2:
                        act.wait_ge(hid_ready, i - 1)
                    nc.scalar.activation(gelu[i % 2][:, 0:cols], bank_h[2 * c][:, 0:cols],
                                         ACT.Gelu).then_inc(gelu_ready, 1)
                    if c == 0 and s + 1 < S and steps[s + 1][3] is not None:
                        split_gathered(s + 1)
                    for piece in pieces_at.get((s, c), []):
                        attention_piece(*piece)
                if s >= 1:
                    evacuate(s - 1)
            evacuate(S - 1)
            for piece in pieces_at.get("end", []):
                attention_piece(*piece)

        @block.vector
        def _(dve):
            count = [0]

            def link(ins):
                count[0] += 1
                ins.then_inc(dve_step, 1)
                dve.wait_ge(dve_step, count[0])

            nc.vector.memset(eps[:], LN_EPS).then_inc(eps_ready, 1)
            nc.vector.memset(val[:, :, D:D + 2], 1.0)

            def statistics(g):
                dve.wait_ge(x_in[g], 16)
                for t in range(g * GROUP, (g + 1) * GROUP):
                    ins = nc.vector.bn_stats(stats[:, t, :], xs[:, t, :])
                link(ins)
                for t in range(g * GROUP, (g + 1) * GROUP):
                    ins = nc.vector.bn_aggr(mv[:, t, :], stats[:, t, :])
                ins.then_inc(mv_ready, 1)

            def normalise(g):
                t0, t1 = g * GROUP, (g + 1) * GROUP
                dve.wait_ge(std1_ready, g + 1)
                link(nc.vector.reciprocal(inv1[:, t0:t1], std1[:, t0:t1]))
                nc.vector.scalar_tensor_tensor(nmi[:, t0:t1], mv[:, t0:t1, 0], -1.0, inv1[:, t0:t1],
                                               ALU.mult, ALU.mult).then_inc(nmi_ready, 1)
                for t in range(t0, t0 + 2):
                    ins = nc.vector.tensor_scalar(xn[:, t, :], xs[:, t, :], mv[:, t, 0:1], inv1[:, t:t + 1],
                                                  ALU.subtract, ALU.mult)
                ins.then_inc(xn_ready, 1)

            statistics(0)
            statistics(1)
            normalise(0)
            statistics(2)
            normalise(1)
            dve.wait_ge(small_in, 16 * 5)
            nc.vector.tensor_copy(beta_cols, beta_sb[:, 0:1].broadcast_to((P, P))).then_inc(wsmall_ready, 1)
            statistics(3)
            normalise(2)
            normalise(3)
            link(nc.vector.tensor_tensor(var2[:, :], mv[:, :, 1], inv1[:, :], ALU.mult))
            nc.vector.tensor_tensor(var2[:, :], var2[:, :], inv1[:, :], ALU.mult).then_inc(var2_ready, 1)
            def first_sum(g):
                dve.wait_ge(xn_ready, g + 1)
                dve.wait_ge(xn_act_ready, g + 1)
                nc.vector.tensor_tensor(acc[:, g * GROUP:(g + 1) * GROUP, :], xs[:, g * GROUP:(g + 1) * GROUP, :],
                                        xn[:, g * GROUP:(g + 1) * GROUP, :], ALU.add).then_inc(acc_ready, 1)

            for g in range(G - 1):
                first_sum(g)
            dve.wait_ge(std2_ready, 1)
            nc.vector.reciprocal(inv2[:, :], std2[:, :]).then_inc(ones_ready, 1)
            link(nc.vector.tensor_scalar(wqkv_g, wqkv_sb[:, :], gamma_sb[:, 0:1], None, ALU.mult))
            link(nc.vector.tensor_copy(wqkv_hi[:, :], wqkv_g))
            nc.vector.tensor_tensor(wqkv_lo[:, :], wqkv_g, wqkv_hi[:, :].bitcast(F32),
                                    ALU.subtract).then_inc(wsmall_ready, 1)

            first_sum(G - 1)
            for g in range(LO_EARLY, G):
                dve.wait_ge(xT_hi_ready, g + 1)
                nc.vector.tensor_tensor(xT_lo[:, g * 512:(g + 1) * 512], xT[:, g * 512:(g + 1) * 512],
                                        xT_hi[:, g * 512:(g + 1) * 512].bitcast(F32),
                                        ALU.subtract).then_inc(xT_late_ready, 1)

            def over_experts(ap):
                return ap.unsqueeze(2).broadcast_to((P, T, E))

            dve.wait_ge(const_ready, 1)
            dve.wait_ge(logits_ready, 1)
            scores = logits = bank_y[:, 0:T * E].rearrange("p (t e) -> p t e", e=E)
            for k in range(TOP_K):
                link(nc.vector.tensor_reduce(top[k][:, :], scores, AX.X, ALU.max))
                link(nc.vector.tensor_tensor(eq[:, :, :], scores, over_experts(top[k][:, :]), ALU.is_equal))
                link(nc.vector.tensor_tensor(eq[:, :, :], eq[:, :, :], rank[:, :, :], ALU.mult))
                link(nc.vector.tensor_reduce(best[:, :], eq[:, :, :], AX.X, ALU.max))
                link(nc.vector.tensor_tensor(chosen[:, k, :, :], eq[:, :, :], over_experts(best[:, :]), ALU.is_equal))
                if k == 0:
                    link(nc.vector.scalar_tensor_tensor(rest[:, :, :], chosen[:, 0, :, :], -3e38, logits,
                                                        ALU.mult, ALU.add))
                    scores = rest[:, :, :]
            nc.vector.tensor_tensor(assigned[:, :, :], chosen[:, 0, :, :], chosen[:, 1, :, :],
                                    ALU.add).then_inc(assigned_ready, 1)
            nc.vector.tensor_tensor(gap[:, :], top[1][:, :], top[0][:, :], ALU.subtract).then_inc(gap_ready, 1)
            dve.wait_ge(before_ready, 1)
            before = bank_y[:, 128:128 + T * E].rearrange("p (t e) -> p t e", e=E)
            nc.vector.tensor_scalar(drop[:, :, :], before, float(CAP), DROPPED, ALU.is_ge, ALU.mult)
            link(nc.vector.tensor_tensor(slot_all[:, :, :], before, first_slot[:, :, :], ALU.add))
            link(nc.vector.tensor_tensor(slot_all[:, :, :], slot_all[:, :, :], drop[:, :, :], ALU.add))
            link(nc.vector.tensor_tensor(picked[:, :, :, :].rearrange("p k t e -> p k (t e)"),
                                         chosen[:, :, :, :].rearrange("p k t e -> p k (t e)"),
                                         slot_all[:, :, :].rearrange("p t e -> p (t e)").unsqueeze(1).broadcast_to((P, TOP_K, T * E)),
                                         ALU.mult))
            link(nc.vector.tensor_reduce(slot[:, :, :], picked[:, :, :, :], AX.X, ALU.add))
            link(nc.vector.tensor_copy(slot_i[:, :, :], slot[:, :, :]))
            nc.vector.tensor_scalar(tile_i[:, :, :], slot_i[:, :, :], 7, None, ALU.arith_shift_right)
            link(nc.vector.tensor_scalar(row_i[:, :, :], slot_i[:, :, :], P - 1, None, ALU.bitwise_and))
            nc.vector.tensor_copy(tile_16[:, :, :], tile_i[:, :, :])
            link(nc.vector.tensor_copy(row_16[:, :, :], row_i[:, :, :]))
            link(nc.vector.tensor_tensor(hot_tile[:, :, :],
                                         tile_16[:, :, :].rearrange("p k t -> p (k t)").unsqueeze(1).broadcast_to((P, RT, KT)),
                                         iota_tiles[:, :, :], ALU.is_equal))
            nc.vector.tensor_tensor(hot_token[:, :, :], hot_tile[:, :, :],
                                    token_id[:, :, :].rearrange("p k t -> p (k t)").unsqueeze(1).broadcast_to((P, RT, KT)),
                                    ALU.mult)
            nc.vector.tensor_tensor(hot_row[:, :, :],
                                    row_16[:, :, :].rearrange("p k t -> p (k t)").unsqueeze(1).broadcast_to((P, P, KT)),
                                    iota_rows[:, :, :], ALU.is_equal).then_inc(hot_ready, 1)
            nc.vector.tensor_scalar(fetch[:, :, :], slot[:, :, :], float(R * CAP - 1), None,
                                    ALU.min).then_inc(fetch_ready, 1)
            nc.vector.tensor_scalar(kept_routed[:, :, :], slot[:, :, :], float(R * CAP), None, ALU.is_lt)
            dve.wait_ge(slots_ready, 1)
            nc.vector.tensor_copy(slot_token[:, :], bank_a[:, 384:384 + RT]).then_inc(list_ready, 1)
            nc.vector.tensor_scalar(kept[:, :, :], before, float(CAP), None, ALU.is_lt)
            dve.wait_ge(gap_exp_ready, 1)
            link(nc.vector.tensor_scalar(gate_sum[:, :], gap_exp[:, :], 1.0, None, ALU.add))
            link(nc.vector.reciprocal(gate[0][:, :], gate_sum[:, :]))
            link(nc.vector.tensor_tensor(gate[1][:, :], gate[0][:, :], gap_exp[:, :], ALU.mult))
            for k in range(TOP_K):
                nc.vector.tensor_tensor(gate_routed[k][:, :], gate[k][:, :], kept_routed[:, k, :], ALU.mult)
            link(nc.vector.tensor_tensor(gate_dense[:, :, :], chosen[:, 0, :, :], over_experts(gate[0][:, :]), ALU.mult))
            link(nc.vector.tensor_tensor(gate_part[:, :, :], chosen[:, 1, :, :], over_experts(gate[1][:, :]), ALU.mult))
            link(nc.vector.tensor_tensor(gate_dense[:, :, :], gate_dense[:, :, :], gate_part[:, :, :], ALU.add))
            nc.vector.tensor_tensor(gate_dense[:, :, :], gate_dense[:, :, :], kept[:, :, :], ALU.mult)

            def queries_keys(u):
                dve.wait_ge(exp_ready, u + 1)
                nc.vector.scalar_tensor_tensor(pre[:, 2 * u:2 * u + 2, :], expo[:, 2 * u:2 * u + 2, :], 1.0,
                                               pre[:, 2 * u:2 * u + 2, :], ALU.min, ALU.add).then_inc(qk_ready, 1)

            dve.wait_ge(bias_ready, 1)
            for t in range(PRE_POOL, T):
                dve.wait_ge(qkv_raw, t + 1)
                nc.vector.scalar_tensor_tensor(pre[:, t, :], bank_h[t % 4][:, 0:2 * D], inv2[:, t:t + 1],
                                               bias[:, 0:2 * D], ALU.mult, ALU.add).then_inc(pre_late_ready, 1)
                if t % 2 == 1:
                    queries_keys((t - PRE_POOL) // 2)
            for u in range((T - PRE_POOL) // 2, U):
                queries_keys(u)
            for b in range(B):
                dve.wait_ge(kv_added, (b + 1) * TB)
                bank = (bank_a, bank_y)[b]
                link(nc.vector.tensor_scalar(v_bias[b], bias[:, 2 * D:QKV], bank[:, D:D + 1], None, ALU.mult))
                link(nc.vector.tensor_tensor(v_bias[b], v_bias[b], bank[:, 0:D], ALU.add))
                nc.vector.tensor_tensor(state[b][:, 0:D], v_bias[b], head_block[:, :], ALU.mult)
                nc.vector.tensor_scalar(state[b][:, D:KVW], head_cols[:, :], bank[:, D:D + 1], None,
                                        ALU.mult).then_inc(state_ready, 1)
            sums = [0]

            def lower_w1(e):
                dve.wait_ge(w1_in[e // 2], 16)
                link(nc.vector.tensor_copy(w1_hi[:, e, :], w1_raw[:, e, :]))
                nc.vector.tensor_tensor(w1_lo[:, e, :], w1_raw[:, e, :], w1_hi[:, e, :].bitcast(F32),
                                        ALU.subtract).then_inc(w1_late_ready, 1)

            for e in range(W1_EARLY, DENSE + 2):
                lower_w1(e)

            def before_sum(tiles):
                if sums[0] == 0:
                    dve.wait_ge(acc_ready, G)
                elif earlier_sum(sums[0], tiles):
                    dve.wait_ge(acc_added, earlier_sum(sums[0], tiles))
                sums[0] += 1

            def add_fetched(n):
                t, k = n // TOP_K, n % TOP_K
                dve.wait_ge(fetched_in[n // 4], 16 * 4)
                before_sum((t,))
                nc.vector.scalar_tensor_tensor(acc[:, t, :], fetched[:, n, :], gate_routed[k][:, t:t + 1],
                                               acc[:, t, :], ALU.mult, ALU.add).then_inc(acc_added, 1)

            def attention_piece(kind, u):
                if kind == "numerators":
                    dve.wait_ge(att_raw, u + 1)
                    both = bank_a[:, 0:2 * KVW].rearrange("p (t c) -> p t c", t=2)
                    link(nc.vector.tensor_scalar(den[:, :, :], both[:, :, D:KVW], DENOM_EPS, None, ALU.add))
                    link(nc.vector.reciprocal(den_inv[:, :, :], den[:, :, :]))
                    if u >= 2:
                        dve.wait_ge(attT_raw, u - 1)
                    for i in range(2):
                        ins = nc.vector.tensor_tensor(
                            att[u % 2][:, i, :].rearrange("p (h c) -> p h c", h=HEADS),
                            both[:, i, 0:D].rearrange("p (h c) -> p h c", h=HEADS),
                            den_inv[:, i, :].unsqueeze(2).broadcast_to((P, HEADS, HD)), ALU.mult)
                    ins.then_inc(att_ready, 1)
                elif kind == "projection":
                    dve.wait_ge(proj_raw, u + 1)
                    before_sum((2 * u, 2 * u + 1))
                    nc.vector.tensor_tensor(acc[:, 2 * u:2 * u + 2, :], acc[:, 2 * u:2 * u + 2, :],
                                            bank_x[1][:, 0:2 * D].rearrange("p (t d) -> p t d", t=2),
                                            ALU.add).then_inc(acc_added, 1)

            def split_gathered(s):
                r = steps[s][3]
                cols = steps[s][2] * P
                dve.wait_ge(xg_hi_ready, r + 1)
                nc.vector.tensor_tensor(xg_lo[r % 2][:, 0:cols], bank_x[0][:, 0:cols],
                                        xg_hi[r % 2][:, 0:cols].bitcast(F32),
                                        ALU.subtract).then_inc(xg_lo_ready, 1)

            def add_dense(s):
                e, t0, nt, r = steps[s]
                if r is not None:
                    return
                dve.wait_ge(down_done, s + 1)
                for j in range(nt):
                    before_sum((t0 + j,))
                    nc.vector.scalar_tensor_tensor(
                        acc[:, t0 + j, :], bank_y[:, j * D:(j + 1) * D], gate_dense[:, t0 + j, e:e + 1],
                        acc[:, t0 + j, :], ALU.mult, ALU.add).then_inc(acc_added, 1)

            if steps[0][3] is not None:
                split_gathered(0)
            for s in range(S):
                cols = steps[s][2] * P
                for c in range(FC):
                    i = FC * s + c
                    dve.wait_ge(gelu_ready, i + 1)
                    if c == 0 and s >= 2:
                        dve.wait_ge(down_done, s - 1)
                    nc.vector.tensor_tensor(hid[s % 2][:, c, 0:cols], gelu[i % 2][:, 0:cols],
                                            bank_h[2 * c + 1][:, 0:cols], ALU.mult).then_inc(hid_ready, 1)
                    if c == 0 and s + 1 < S and steps[s + 1][3] is not None:
                        split_gathered(s + 1)
                    for piece in pieces_at.get((s, c), []):
                        attention_piece(*piece)
                    for n in fetched_at.get((s, c), []):
                        add_fetched(n)
                if s + 1 < S and steps[s + 1][3] is not None:
                    if steps[s + 1][1] == 0 and DENSE + 2 <= steps[s + 1][0] + 1 < E:
                        lower_w1(steps[s + 1][0] + 1)
                if s >= 1:
                    add_dense(s - 1)
            add_dense(S - 1)
            for piece in pieces_at.get("end", []):
                attention_piece(*piece)

            for n in fetched_at.get("end", []):
                add_fetched(n)

        @block.tensor
        def _(pe):
            def product(dst, halves, last=None):
                (a_hi, a_lo), (b_hi, b_lo) = halves
                nc.tensor.matmul(dst, a_lo, b_hi, start=True, stop=False)
                nc.tensor.matmul(dst, a_hi, b_lo, start=False, stop=False)
                return nc.tensor.matmul(dst, a_hi, b_hi, start=False, stop=True)

            def x_halves(t):
                return xT_hi[:, t * P:(t + 1) * P], xT_lo[:, t * P:(t + 1) * P]

            def transpose_group(g):
                pe.wait_ge(xn_ready, g + 1)
                pe.wait_ge(xn_act_ready, g + 1)
                if g >= 2:
                    pe.wait_ge(xT_ready, g - 1)
                for j in range(GROUP):
                    ins = nc.tensor.transpose(bank_x[g % 2][:, j * P:(j + 1) * P], xn[:, g * GROUP + j, :],
                                              ident[:, :])
                ins.then_inc(xT_raw, 1)

            def logits_group(g):
                pe.wait_ge(xT_ready, g + 1)
                for t in range(g * GROUP, (g + 1) * GROUP):
                    ins = nc.tensor.matmul(bank_y[:, t * E:(t + 1) * E], xT[:, t * P:(t + 1) * P], wg_sb[:, :],
                                           start=True, stop=True)
                if g == G - 1:
                    ins.then_inc(logits_ready, 1)

            pe.wait_ge(ident_ready, 1)
            transpose_group(0)
            transpose_group(1)
            pe.wait_ge(wsmall_ready, 1)
            logits_group(0)
            transpose_group(2)
            logits_group(1)
            transpose_group(3)
            logits_group(2)
            logits_group(3)
            nc.tensor.matmul(bank_a[:, 0:QKV], beta_cols, wqkv_sb[:, :],
                             start=True, stop=True).then_inc(bias_raw, 1)

            def qkv_tile(t):
                g = t // GROUP
                if g < LO_EARLY:
                    pe.wait_ge(xT_lo_ready, g + 1)
                else:
                    pe.wait_ge(xT_late_ready, g - LO_EARLY + 1)
                if t >= 4:
                    pe.wait_ge(val_ready, t - 3)
                product(bank_h[t % 4][:, 0:QKV], (x_halves(t), (wqkv_hi[:, :], wqkv_lo[:, :]))).then_inc(qkv_raw, 1)

            pe.wait_ge(wsmall_ready, 2)
            for t in range(4):
                qkv_tile(t)
            pe.wait_ge(const_ready, 1)
            pe.wait_ge(assigned_ready, 1)
            before = bank_y[:, 128:128 + T * E]
            nc.tensor.matmul(before, earlier[:, :], assigned[:, :, :], start=True, stop=False)
            for t in range(T - 1):
                ins = nc.tensor.matmul(before[:, (t + 1) * E:].rearrange("p (t e) -> p t e", e=E), ones_bf[:, :],
                                       assigned[:, t:t + 1, :].broadcast_to((P, T - 1 - t, E)),
                                       start=False, stop=(t == T - 2))
            ins.then_inc(before_ready, 1)
            for t in range(4, PRE_POOL):
                qkv_tile(t)
            pe.wait_ge(bias_ready, 1)
            pe.wait_ge(hot_ready, 1)
            for n in range(KT):
                ins = nc.tensor.matmul(bank_a[:, 384:384 + RT], hot_row[:, :, n], hot_token[:, :, n],
                                       start=(n == 0), stop=(n == KT - 1))
            ins.then_inc(slots_ready, 1)
            for t in range(PRE_POOL, T):
                qkv_tile(t)

            def transpose_queries(t):
                if t % GROUP == 0 and t >= 2 * GROUP:
                    pe.wait_ge(qT_ready, t // GROUP - 1)
                return nc.tensor.transpose(bank_x[(t // GROUP) % 2][:, (t % GROUP) * P:(t % GROUP + 1) * P],
                                           pre[:, t, 0:D], ident[:, :])

            for t in range(T):
                pe.wait_ge(qk_ready, t // 2 + 1)
                pe.wait_ge(val_ready, t + 1)
                if t == 0:
                    pe.wait_ge(list_ready, 1)
                ins = transpose_queries(t)
                if t % GROUP == GROUP - 1:
                    ins.then_inc(qT_raw, 1)
                b = t // TB
                nc.tensor.matmul((bank_a, bank_y)[b][:, 0:D + 2], pre[:, t, D:2 * D], val[:, t, :],
                                 start=(t % TB == 0), stop=(t % TB == TB - 1)).then_inc(kv_added, 1)

            def attention_piece(kind, u):
                if kind == "numerators":
                    pe.wait_ge(state_ready, 2 * u // TB + 1)
                    if u == 0:
                        pe.wait_ge(qT_ready, G)
                    if u >= 1:
                        pe.wait_ge(att_ready, u)
                    for i in range(2):
                        t = 2 * u + i
                        ins = nc.tensor.matmul(bank_a[:, i * KVW:(i + 1) * KVW], qT[:, t * P:(t + 1) * P],
                                               state[t // TB][:, :], start=True, stop=True)
                    ins.then_inc(att_raw, 1)
                elif kind == "transposes":
                    pe.wait_ge(att_ready, u + 1)
                    if u >= 1:
                        pe.wait_ge(acc_added, sums_with["projection", u - 1])
                    for i in range(2):
                        ins = nc.tensor.transpose(bank_x[1][:, i * P:(i + 1) * P], att[u % 2][:, i, :], ident[:, :])
                    ins.then_inc(attT_raw, 1)
                else:
                    pe.wait_ge(attT_ready, u + 1)
                    for i in range(2):
                        ins = nc.tensor.matmul(bank_x[1][:, i * D:(i + 1) * D], attT[u % 2][:, i * P:(i + 1) * P],
                                               wout_sb[:, :], start=True, stop=True)
                    ins.then_inc(proj_raw, 1)

            def transpose_slots(s):
                e, j0, nj, r = steps[s]
                if j0 == 0:
                    pe.wait_ge(rows_in[e - DENSE], 16 * ST)
                if r >= 1:
                    pe.wait_ge(xg_lo_ready, r)
                for j in range(nj):
                    n = (e - DENSE) * ST + j0 + j
                    ins = nc.tensor.transpose(bank_x[0][:, j * P:(j + 1) * P], gathered[:, n, :], ident[:, :])
                ins.then_inc(xg_raw, 1)

            def up(s):
                e, j0, nj, r = steps[s]
                cols = nj * P
                if r is None:
                    right = xT_hi[:, j0 * P:j0 * P + cols], xT_lo[:, j0 * P:j0 * P + cols]
                else:
                    pe.wait_ge(xg_lo_ready, r + 1)
                    right = xg_hi[r % 2][:, 0:cols], xg_lo[r % 2][:, 0:cols]
                if e < W1_EARLY:
                    pe.wait_ge(w1_lo_ready, e + 1)
                else:
                    pe.wait_ge(w1_late_ready, e - W1_EARLY + 1)
                for c in range(FC):
                    if c == 1 and s + 1 < S and steps[s + 1][3] is not None:
                        transpose_slots(s + 1)
                    if s >= 1:
                        pe.wait_ge(gelu_ready, FC * (s - 1) + c + 1)
                        pe.wait_ge(hid_ready, FC * (s - 1) + c + 1)
                    for i, first in enumerate((c * P, F + c * P)):
                        left = w1_hi[:, e, first:first + P], w1_lo[:, e, first:first + P]
                        ins = product(bank_h[2 * c + i][:, 0:cols], (left, right))
                    ins.then_inc(up_done, 1)
                    for piece in pieces_at.get((s, c), []):
                        attention_piece(*piece)

            def down(s):
                e, _, nj, _ = steps[s]
                pe.wait_ge(hid_ready, FC * (s + 1))
                if s >= 1:
                    if steps[s - 1][3] is not None:
                        pe.wait_ge(y_evac, steps[s - 1][3] + 1)
                    else:
                        pe.wait_ge(acc_added, sums_with["step", s - 1])
                else:
                    pe.wait_ge(state_ready, B)
                pe.wait_ge(w2_in[min(e // 2, 1)], 16)
                for j in range(nj):
                    for c in range(FC):
                        ins = nc.tensor.matmul(bank_y[:, j * D:(j + 1) * D], hid[s % 2][:, c, j * P:(j + 1) * P],
                                               w2_sb[:, e, c, :], start=(c == 0), stop=(c == FC - 1))
                ins.then_inc(down_done, 1)

            pe.wait_ge(val_ready, T)
            pe.wait_ge(qT_ready, G)
            if steps[0][3] is not None:
                transpose_slots(0)
            for s in range(S):
                up(s)
                if s >= 1:
                    down(s - 1)
            down(S - 1)
            for piece in pieces_at.get("end", []):
                attention_piece(*piece)


def kernel(L0_attn_x, L0_attn_gamma, L0_attn_beta, L0_attn_Wqkv, L0_attn_Wout, L0_ffn_Wg, L0_ffn_W1, L0_ffn_W2):
    import numpy as np
    import concourse.bacc as bacc
    from concourse.bass_utils import run_bass_kernel_spmd

    laid_out = {
        "x": L0_attn_x,
        "gamma": np.asarray(L0_attn_gamma).reshape(-1, 1),
        "beta": np.asarray(L0_attn_beta).reshape(-1, 1),
        "wqkv": L0_attn_Wqkv,
        "wout": L0_attn_Wout,
        "wg_t": np.asarray(L0_ffn_Wg).T,
        "w1": L0_ffn_W1,
        "w2": L0_ffn_W2,
    }
    nc = bacc.Bacc("TRN2", target_bir_lowering=False, num_devices=1)
    arrays, args = {}, []
    for name, a in laid_out.items():
        a = np.ascontiguousarray(a)
        arrays[f"in_{name}"] = a
        args.append(nc.dram_tensor(f"in_{name}", a.shape, mybir.dt.from_np(a.dtype), kind="ExternalInput").ap())
    shape = np.asarray(L0_attn_x).shape
    args.append(nc.dram_tensor("out_block", shape, F32, kind="ExternalOutput").ap())
    moe_attention_block(nc, *args)
    r = run_bass_kernel_spmd(nc, [arrays], core_ids=[0])
    return r.results[0]["out_block"]
```

```python
from contextlib import ExitStack

import concourse.bass as bass
from concourse import mybir

F32 = mybir.dt.float32
F32R = mybir.dt.float32r
F16 = mybir.dt.float16
BF16 = mybir.dt.bfloat16
I32 = mybir.dt.int32
ALU = mybir.AluOpType
ACT = mybir.ActivationFunctionType
AX = mybir.AxisListType

P = 128
LN_EPS = 1e-5
DENOM_EPS = 1e-6
HEADS = 16
TOP_K = 2
CAPACITY_FACTOR = 1.25
GROUP = 4
DENSE = 1
EARLY = 2
DENSE_AFTER = (7, 7)
ATT_FROM = 36
ATT_EVERY = 2
ATT_DENSE = 14
GATHERS_AHEAD = 5
LO_EARLY = 2
EARLY_SUMS = 2
KV_LAG = 8
RESULTS_AT = 2
SLOTS_AT = 4
LIST_AT = 2
PRE_POOL = 2
DROPPED = 8192.0
PARTS = ((0, 3), (3, 2))


def moe_attention_block(nc, x, gamma, beta, wqkv, wout, wg_t, w1, w2, out):
    B, L, D = x.shape
    N = B * L
    E, _, F2 = w1.shape
    F = F2 // 2
    T = N // P
    G = T // GROUP
    TB = L // P
    CAP = int(N * TOP_K * CAPACITY_FACTOR / E)
    ST = CAP // P
    R = E - DENSE
    RT = R * ST
    HD = D // HEADS
    FC = F // P
    QKV = 3 * D
    KVW = D + HEADS
    assert D == P and CAP % P == 0 and sum(n for _, n in PARTS) == ST and N <= 2048 and FC == 2

    routed_steps = [(e, j0, nj) for e in range(DENSE, E) for j0, nj in PARTS]
    all_token_steps = [(e, g * GROUP, GROUP, None) for e in range(DENSE) for g in range(G)]
    steps = []
    for r, (e, j0, nj) in enumerate(routed_steps):
        steps.append((e, j0, nj, r))
        if (r + 1) % len(PARTS) == 0:
            steps += [step for step, after in zip(all_token_steps[EARLY:], DENSE_AFTER)
                      if after == (r + 1) // len(PARTS)]
    assert EARLY + len(steps) == len(routed_steps) + len(all_token_steps)
    S = len(steps)
    step_of_routed = [s for s in range(S) if steps[s][3] is not None]
    dense_steps = [s for s in range(S) if steps[s][3] is None]
    U = T // 2
    KT = TOP_K * T
    pieces = [[("queries", g)] for g in range(G)]
    for u in range(U + 2):
        pieces.append(([("transposes", u - 1)] if 0 <= u - 1 < U else [])
                      + ([("numerators", u)] if u < U else [])
                      + ([("projection", u - 2)] if u >= 2 else []))
    hurried = [s for s in range(1, S) if steps[s - 1][3] is not None and steps[s][3] is None][-1]
    spots = [(s, c, i) for s in range(S) for c in range(FC) for i in range(2)]
    chunks = [(s, c) for s in range(S) for c in range(FC)]
    pieces_at = {}
    i = ATT_FROM
    for piece in pieces:
        pieces_at.setdefault(spots[i] if i < len(spots) else "end", []).extend(piece)
        i += ATT_EVERY if i < 2 * FC * ATT_DENSE else 1
    sum_tiles, sums_with = [], {}

    def note_sum(name, tiles):
        sum_tiles.append(tiles)
        sums_with[name] = len(sum_tiles)

    for s, c in chunks:
        assert not pieces_at.get((s, c, 0)) or s >= EARLY_SUMS + EARLY
        if c == 0 and EARLY_SUMS <= s < EARLY_SUMS + EARLY:
            for j in range(GROUP):
                note_sum(("early", s - EARLY_SUMS), (all_token_steps[s - EARLY_SUMS][1] + j,))
        for kind, u in pieces_at.get((s, c, 0), []) + pieces_at.get((s, c, 1), []):
            if kind == "projection":
                note_sum((kind, u), (2 * u, 2 * u + 1))
        if s >= 1 and c == FC - 1 and steps[s - 1][3] is None:
            for j in range(GROUP):
                note_sum(("step", s - 1), (steps[s - 1][1] + j,))
    for kind, u in pieces_at.get("end", []):
        if kind == "projection":
            note_sum((kind, u), (2 * u, 2 * u + 1))
    assert steps[-1][1] == T - GROUP and steps[-1][3] is None
    for t in range(0, T, 2):
        if t == T - GROUP:
            for j in range(GROUP):
                note_sum(("step", S - 1), (t + j,))
        for k in range(TOP_K):
            note_sum(("fetched", t, k), (t,))

    def earlier_sum(index, tiles):
        return max([i + 1 for i in range(index) if set(sum_tiles[i]) & set(tiles)], default=0)

    x_tiles = x.rearrange("b (t p) d -> p (b t) d", p=P)
    out_tiles = out.rearrange("b (t p) d -> p (b t) d", p=P)
    xn_rows = nc.dram_tensor("xn_rows", [N, D], F32).ap()
    y_rows = nc.dram_tensor("y_rows", [TOP_K * N + R * CAP, D], F32).ap()
    xn_rows_tiles = xn_rows.rearrange("(t p) d -> p t d", p=P)
    y_rows_tiles = y_rows[0:TOP_K * N, :].rearrange("(t p) d -> p t d", p=P)

    with ExitStack() as ctx:
        def sb(name, shape, dt=F32):
            return ctx.enter_context(nc.sbuf_tensor(name, shape, dt))

        def sem(name):
            return ctx.enter_context(nc.semaphore(name))

        xs = sb("xs", [P, T, D])
        acc = xs
        xn = sb("xn", [P, T, D])
        xT_hi = sb("xT_hi", [P, N], F32R)
        xT_lo = sb("xT_lo", [P, N], F32R)
        w1_raw = sb("w1_raw", [P, E, F2])
        w1_hi = sb("w1_hi", [P, E, F2], F32R)
        w1_lo = sb("w1_lo", [P, E, F2], F32R)
        w2_sb = sb("w2_sb", [P, E, FC, D])
        wqkv_sb = sb("wqkv_sb", [P, QKV])
        wqkv_hi = sb("wqkv_hi", [P, QKV], F32R)
        wqkv_lo = sb("wqkv_lo", [P, QKV], F32R)
        wout_sb = sb("wout_sb", [P, D])
        wg_sb = sb("wg_sb", [P, E])
        gamma_sb = sb("gamma_sb", [P, 1])
        beta_sb = sb("beta_sb", [P, 1])
        bias = sb("bias", [P, QKV])

        ident = sb("ident", [P, P])
        earlier = sb("earlier", [P, P], BF16)
        ones_bf = sb("ones_bf", [P, P], BF16)
        head_block = sb("head_block", [P, D])
        head_cols = sb("head_cols", [P, HEADS])
        iota_tiles = sb("iota_tiles", [P, RT, KT], F16)
        token_id = sb("token_id", [P, TOP_K, T], F16)
        first_slot = sb("first_slot", [P, T, E])
        rank = sb("rank", [P, T, E])
        eps = sb("eps", [P, 1])
        unused = sb("unused", [P, 1])
        unused_gelu = sb("unused_gelu", [P, 1])

        stats = sb("stats", [P, T, 6])
        mv = sb("mv", [P, T, 2])
        std1 = sb("std1", [P, T])
        inv1 = sb("inv1", [P, T])
        nmi = sb("nmi", [P, T])
        var2 = sb("var2", [P, T])
        std2 = sb("std2", [P, T])
        inv2 = sb("inv2", [P, T])

        logit = sb("logit", [P, T, E])
        rest = sb("rest", [P, T, E])
        eq = sb("eq", [P, T, E])
        chosen = sb("chosen", [P, TOP_K, T, E])
        top = [sb(f"top{k}", [P, T]) for k in range(TOP_K)]
        best = sb("best", [P, T])
        gap = sb("gap", [P, T])
        gap_exp = sb("gap_exp", [P, T])
        gate_sum = sb("gate_sum", [P, T])
        gate = [sb(f"gate{k}", [P, T]) for k in range(TOP_K)]
        gate_routed = [sb(f"gate_routed{k}", [P, T]) for k in range(TOP_K)]
        assigned = sb("assigned", [P, T, E], BF16)
        kept = sb("kept", [P, T, E])
        slot_all = sb("slot_all", [P, T, E])
        drop = sb("drop", [P, T, E])
        picked = sb("picked", [P, TOP_K, T, E])
        slot = sb("slot", [P, TOP_K, T])
        slot_i = sb("slot_i", [P, TOP_K, T], I32)
        row_i = sb("row_i", [P, TOP_K, T], I32)
        tile_i = sb("tile_i", [P, TOP_K, T], I32)
        row_16 = sb("row_16", [P, TOP_K, T], F16)
        tile_16 = sb("tile_16", [P, TOP_K, T], F16)
        kept_routed = sb("kept_routed", [P, TOP_K, T])
        no_token = sb("no_token", [P, RT])
        vacant = sb("vacant", [P, RT])
        choices = sb("choices", [P, RT])
        target = sb("target", [P, RT])
        slot_target = sb("slot_target", [P, RT], I32)
        zeros = sb("zeros", [P, D])
        gate_dense = sb("gate_dense", [P, T, E])
        gate_part = sb("gate_part", [P, T, E])
        hot = sb("hot", [P, 2 * RT, KT], F16)
        hot_token, hot_tile = hot[:, 0:RT, :], hot[:, RT:2 * RT, :]
        slot_token = sb("slot_token", [P, RT], I32)

        gathered = sb("gathered", [P, RT, D])
        iota_rows = gathered[:, :, :].rearrange("p n d -> p (n d)")[:, 0:P * KT // 2] \
            .bitcast(F16).rearrange("p (r n) -> p r n", n=KT)
        xg_hi = [sb(f"xg_hi{i}", [P, 3 * P], F32R) for i in range(2)]
        xg_lo = [sb(f"xg_lo{i}", [P, 3 * P], F32R) for i in range(2)]
        y_early = sb("y_early", [P, EARLY, GROUP * P])
        gelu = [sb(f"gelu{i}", [P, GROUP * P]) for i in range(2)]
        hid = [sb(f"hid{i}", [P, FC, GROUP * P]) for i in range(2)]

        pre = sb("pre", [P, T, 2 * D])
        wqkv_g, beta_cols = (pre[:, 0:2, :].rearrange("p t n -> p (t n)")[:, a:b] for a, b in ((0, QKV), (QKV, QKV + P)))
        xT = pre[:, T // 2:T, :].rearrange("p t n -> p (t n)")
        val = sb("val", [P, T, D + 2])
        expo = sb("expo", [P, T, 2 * D])
        qT = sb("qT", [P, N])
        hot_row = qT[:, 0:P * KT // 2].bitcast(F16).rearrange("p (r n) -> p r n", n=KT)
        state = [sb(f"state{b}", [P, KVW]) for b in range(B)]
        den = sb("den", [P, 2, HEADS])
        den_inv = sb("den_inv", [P, 2, HEADS])
        att = [sb(f"att{i}", [P, 2, D]) for i in range(2)]
        v_bias = [att[b][:, 0, :] for b in range(B)]
        attT = [sb(f"attT{i}", [P, 2 * P]) for i in range(2)]
        fetched = expo[:, :, :].rearrange("p (k h) c -> p k (h c)", k=TOP_K).rearrange("p k (t d) -> p k t d", d=D)

        bank_x = [ctx.enter_context(nc.psum_tensor(f"bank_x{i}", [P, 512], F32)) for i in range(2)]
        bank_h = [ctx.enter_context(nc.psum_tensor(f"bank_h{i}", [P, 512], F32)) for i in range(4)]
        bank_y = ctx.enter_context(nc.psum_tensor("bank_y", [P, 512], F32))
        bank_a = ctx.enter_context(nc.psum_tensor("bank_a", [P, 512], F32))

        x_in = [sem(f"x_in{g}") for g in range(G)]
        small_in = sem("small_in")
        w1_in = [sem(f"w1_in{i}") for i in range(E // 2)]
        w2_in = [sem(f"w2_in{i}") for i in range(2)]
        xn_stored = sem("xn_stored")
        rows_in = [sem(f"rows_in{e}") for e in range(R)]
        zeros_stored = sem("zeros_stored")
        y_stored = sem("y_stored")
        fetched_in = [sem(f"fetched_in{g}") for g in range(G)]
        out_stored = sem("out_stored")
        ident_ready = sem("ident_ready")
        const_ready = sem("const_ready")
        pool_step = sem("pool_step")
        dve_step = sem("dve_step")
        eps_ready = sem("eps_ready")
        mv_ready = sem("mv_ready")
        std1_ready = sem("std1_ready")
        nmi_ready = sem("nmi_ready")
        xn_ready = sem("xn_ready")
        xn_act_ready = sem("xn_act_ready")
        xT_raw = sem("xT_raw")
        xT_hi_ready = sem("xT_hi_ready")
        xT_lo_ready = sem("xT_lo_ready")
        xT_late_ready = sem("xT_late_ready")
        xT_ready = sem("xT_ready")
        wsmall_ready = sem("wsmall_ready")
        logits_ready = sem("logits_ready")
        acc_ready = sem("acc_ready")
        w1_hi_ready = sem("w1_hi_ready")
        w1_lo_ready = sem("w1_lo_ready")
        gap_ready = sem("gap_ready")
        gap_exp_ready = sem("gap_exp_ready")
        assigned_ready = sem("assigned_ready")
        before_ready = sem("before_ready")
        hot_ready = sem("hot_ready")
        slots_ready = sem("slots_ready")
        list_ready = sem("list_ready")
        target_ready = sem("target_ready")
        zeros_ready = sem("zeros_ready")
        gates_ready = sem("gates_ready")
        ones_ready = sem("ones_ready")
        bias_raw = sem("bias_raw")
        bias_ready = sem("bias_ready")
        var2_ready = sem("var2_ready")
        std2_ready = sem("std2_ready")
        qkv_raw = sem("qkv_raw")
        scaled_ready = sem("scaled_ready")
        pre_ready = sem("pre_ready")
        pre_late_ready = sem("pre_late_ready")
        val_ready = sem("val_ready")
        exp_ready = sem("exp_ready")
        qk_ready = sem("qk_ready")
        kv_added = sem("kv_added")
        qT_raw = sem("qT_raw")
        qT_ready = sem("qT_ready")
        state_ready = sem("state_ready")
        att_raw = sem("att_raw")
        att_ready = sem("att_ready")
        attT_raw = sem("attT_raw")
        attT_ready = sem("attT_ready")
        proj_raw = sem("proj_raw")
        early_up = sem("early_up")
        early_gelu = sem("early_gelu")
        early_hid = sem("early_hid")
        early_down = sem("early_down")
        early_y = sem("early_y")
        xg_raw = sem("xg_raw")
        xg_hi_ready = sem("xg_hi_ready")
        xg_lo_ready = sem("xg_lo_ready")
        up_done = sem("up_done")
        gelu_ready = sem("gelu_ready")
        hid_ready = sem("hid_ready")
        down_done = sem("down_done")
        y_evac = sem("y_evac")
        acc_added = sem("acc_added")
        pool_added = sem("pool_added")
        weighted_ready = sem("weighted_ready")

        block = ctx.enter_context(nc.Block())

        @block.sync
        def _(sp):
            for g in range(G):
                sp.dma_start(xs[:, g * GROUP:(g + 1) * GROUP, :],
                             x_tiles[:, g * GROUP:(g + 1) * GROUP, :]).then_inc(x_in[g], 16)
            for i in range(E // 2):
                sp.dma_start(w1_raw[:, 2 * i:2 * i + 2, :],
                             w1[2 * i:2 * i + 2].rearrange("e p n -> p e n")).then_inc(w1_in[i], 16)
                if i == 0:
                    sp.dma_start(w2_sb[:, 0:2, :, :],
                                 w2[0:2].rearrange("e (c p) d -> p e c d", p=P)).then_inc(w2_in[0], 16)
            sp.dma_start(w2_sb[:, 2:E, :, :],
                         w2[2:E].rearrange("e (c p) d -> p e c d", p=P)).then_inc(w2_in[1], 16)
            sp.wait_ge(zeros_ready, 1)
            for k in range(TOP_K):
                sp.dma_start(y_rows_tiles[:, k * T:(k + 1) * T, :],
                             zeros[:, :].unsqueeze(1).broadcast_to((P, T, D))).then_inc(zeros_stored, 16)
            for g in range(G):
                sp.wait_ge(xn_ready, g + 1)
                sp.wait_ge(xn_act_ready, g + 1)
                sp.dma_start(xn_rows_tiles[:, g * GROUP:(g + 1) * GROUP, :],
                             xn[:, g * GROUP:(g + 1) * GROUP, :]).then_inc(xn_stored, 16)
            sp.wait_ge(y_stored, 16 * RT)
            for g in range(G):
                for k in range(TOP_K):
                    sp.dma_start(fetched[:, k, g * GROUP:(g + 1) * GROUP, :],
                                 y_rows_tiles[:, k * T + g * GROUP:k * T + (g + 1) * GROUP, :]
                                 ).then_inc(fetched_in[g], 16)
            for g in range(G):
                sp.wait_ge(acc_added, earlier_sum(len(sum_tiles), range(g * GROUP, (g + 1) * GROUP)))
                sp.wait_ge(pool_added, (g + 1) * TOP_K)
                sp.dma_start(out_tiles[:, g * GROUP:(g + 1) * GROUP, :],
                             acc[:, g * GROUP:(g + 1) * GROUP, :]).then_inc(out_stored, 16)
            sp.wait_ge(out_stored, 16 * G)

        @block.gpsimd
        def _(pool):
            count = [0]

            def link(ins):
                count[0] += 1
                ins.then_inc(pool_step, 1)
                pool.wait_ge(pool_step, count[0])

            link(nc.gpsimd.memset(ident[:], 0.0))
            nc.gpsimd.affine_select(out=ident[:], in_=ident[:], compare_op=ALU.not_equal, fill=1.0,
                                    base=0, pattern=[[-1, P]], channel_multiplier=1).then_inc(ident_ready, 1)
            link(nc.gpsimd.memset(earlier[:], 1.0))
            nc.gpsimd.affine_select(out=earlier[:], in_=earlier[:], compare_op=ALU.is_gt, fill=0.0,
                                    base=0, pattern=[[1, P]], channel_multiplier=-1)
            nc.gpsimd.memset(ones_bf[:], 1.0)
            link(nc.gpsimd.memset(head_cols[:], 1.0))
            link(nc.gpsimd.affine_select(out=head_cols[:], in_=head_cols[:], compare_op=ALU.is_ge, fill=0.0,
                                         base=0, pattern=[[-HD, HEADS]], channel_multiplier=1))
            link(nc.gpsimd.affine_select(out=head_cols[:], in_=head_cols[:], compare_op=ALU.is_ge, fill=0.0,
                                         base=HD - 1, pattern=[[HD, HEADS]], channel_multiplier=-1))
            nc.gpsimd.tensor_copy(head_block[:, :].rearrange("p (h c) -> p h c", h=HEADS),
                                  head_cols[:, :].unsqueeze(2).broadcast_to((P, HEADS, HD)))
            nc.gpsimd.iota(token_id[:], pattern=[[0, TOP_K], [P, T]], base=0, channel_multiplier=1,
                           allow_small_or_imprecise_dtypes=True)
            nc.gpsimd.memset(zeros[:], 0.0).then_inc(zeros_ready, 1)
            nc.gpsimd.iota(no_token[:], pattern=[[P, RT]], base=(TOP_K + 1) * N, channel_multiplier=1,
                           allow_small_or_imprecise_dtypes=True)
            nc.gpsimd.iota(rank[:], pattern=[[0, T], [-1, E]], base=E, channel_multiplier=0,
                           allow_small_or_imprecise_dtypes=True)
            link(nc.gpsimd.memset(first_slot[:], DROPPED))
            nc.gpsimd.iota(iota_tiles[:], pattern=[[1, RT], [0, KT]], base=0, channel_multiplier=0,
                           allow_small_or_imprecise_dtypes=True)
            nc.gpsimd.iota(iota_rows[:, :, :], pattern=[[1, P], [0, KT]], base=0, channel_multiplier=0,
                           allow_small_or_imprecise_dtypes=True)
            nc.gpsimd.iota(first_slot[:, :, DENSE:E], pattern=[[0, T], [CAP, R]], base=0,
                           channel_multiplier=0, allow_small_or_imprecise_dtypes=True).then_inc(const_ready, 1)

            def lower_w1(e):
                pool.wait_ge(w1_hi_ready, e + 1)
                nc.gpsimd.tensor_tensor(w1_lo[:, e, :], w1_raw[:, e, :], w1_hi[:, e, :].bitcast(F32),
                                        ALU.subtract).then_inc(w1_lo_ready, 1)

            for g in range(LO_EARLY):
                pool.wait_ge(xT_hi_ready, g + 1)
                nc.gpsimd.tensor_tensor(xT_lo[:, g * 512:(g + 1) * 512], xT[:, g * 512:(g + 1) * 512],
                                        xT_hi[:, g * 512:(g + 1) * 512].bitcast(F32),
                                        ALU.subtract).then_inc(xT_lo_ready, 1)
                lower_w1(g)
            for e in range(LO_EARLY, E):
                lower_w1(e)
            pool.wait_ge(bias_ready, 1)
            for t in range(PRE_POOL):
                pool.wait_ge(scaled_ready, t + 1)
                nc.gpsimd.tensor_tensor(pre[:, t, :], pre[:, t, :], bias[:, 0:2 * D],
                                        ALU.add).then_inc(pre_ready, 1)
            pool.wait_ge(xn_stored, 16 * G)
            pool.wait_ge(list_ready, 1)

            def gather(r):
                for n in range(r * ST, (r + 1) * ST):
                    nc.gpsimd.indirect_dma_start(
                        gathered[:, n, :], None, xn_rows,
                        bass.IndirectOffsetOnAxis(ap=slot_token[:, n:n + 1], axis=0),
                    ).then_inc(rows_in[r], 16)

            def scatter(r):
                if r == 0:
                    pool.wait_ge(zeros_stored, 16 * TOP_K)
                    pool.wait_ge(target_ready, 1)
                for i, (j0, nj) in enumerate(PARTS):
                    pool.wait_ge(y_evac, len(PARTS) * r + i + 1)
                    for n in range(r * ST + j0, r * ST + j0 + nj):
                        nc.gpsimd.indirect_dma_start(
                            y_rows, bass.IndirectOffsetOnAxis(ap=slot_target[:, n:n + 1], axis=0),
                            gathered[:, n, :], None,
                        ).then_inc(y_stored, 16)

            for r in range(R):
                gather(r)
                if r + 1 >= GATHERS_AHEAD:
                    scatter(r + 1 - GATHERS_AHEAD)
            for r in range(R + 1 - GATHERS_AHEAD, R):
                scatter(r)
            for g in range(G):
                odd = slice(g * GROUP + 1, (g + 1) * GROUP, 2)
                pool.wait_ge(acc_added, earlier_sum(len(sum_tiles), range(g * GROUP + 1, (g + 1) * GROUP, 2)))
                for k in range(TOP_K):
                    pool.wait_ge(weighted_ready, TOP_K * g + k + 1)
                    if k > 0:
                        pool.wait_ge(pool_added, TOP_K * g + k)
                    nc.gpsimd.tensor_tensor(acc[:, odd, :], acc[:, odd, :], fetched[:, k, odd, :],
                                            ALU.add).then_inc(pool_added, 1)

        @block.scalar
        def _(act):
            act.dma_start(wqkv_sb[:, :], wqkv).then_inc(small_in, 16)
            act.dma_start(wg_sb[:, :], wg_t).then_inc(small_in, 16)
            act.dma_start(gamma_sb[:, :], gamma).then_inc(small_in, 16)
            act.dma_start(beta_sb[:, :], beta).then_inc(small_in, 16)
            act.dma_start(wout_sb[:, :], wout).then_inc(small_in, 16)

            def root(g):
                act.wait_ge(mv_ready, g + 1)
                nc.scalar.activation(std1[:, g * GROUP:(g + 1) * GROUP], mv[:, g * GROUP:(g + 1) * GROUP, 1],
                                     ACT.Sqrt, bias=eps[:, 0:1]).then_inc(std1_ready, 1)

            def normalise(g):
                act.wait_ge(nmi_ready, g + 1)
                for t in range(g * GROUP + 2, (g + 1) * GROUP):
                    ins = nc.scalar.activation(xn[:, t, :], xs[:, t, :], ACT.Identity, scale=inv1[:, t:t + 1],
                                               bias=nmi[:, t:t + 1])
                ins.then_inc(xn_act_ready, 1)

            def transposed(g):
                act.wait_ge(xT_raw, g + 1)
                nc.scalar.activation(xT[:, g * 512:(g + 1) * 512], bank_x[g % 2][:, :],
                                     ACT.Copy).then_inc(xT_ready, 1)

            def upper_transposed(g):
                act.wait_ge(xT_ready, g + 1)
                nc.scalar.activation(xT_hi[:, g * 512:(g + 1) * 512], xT[:, g * 512:(g + 1) * 512],
                                     ACT.Copy).then_inc(xT_hi_ready, 1)

            def upper_w1(i):
                act.wait_ge(w1_in[i], 16)
                for e in (2 * i, 2 * i + 1):
                    nc.scalar.activation(w1_hi[:, e, :], w1_raw[:, e, :], ACT.Copy).then_inc(w1_hi_ready, 1)

            act.wait_ge(eps_ready, 1)
            root(0)
            root(1)
            normalise(0)
            root(2)
            normalise(1)
            transposed(0)
            root(3)
            normalise(2)
            transposed(1)
            normalise(3)
            transposed(2)
            act.wait_ge(var2_ready, 1)
            nc.scalar.activation(std2[:, :], var2[:, :], ACT.Sqrt, bias=eps[:, 0:1]).then_inc(std2_ready, 1)
            upper_transposed(0)
            transposed(3)
            for g in range(1, G):
                upper_transposed(g)
            upper_w1(0)
            act.wait_ge(bias_raw, 1)
            nc.scalar.activation(bias[:, :], bank_a[:, 0:QKV], ACT.Copy).then_inc(bias_ready, 1)
            upper_w1(1)
            for i in range(EARLY):
                for c in range(FC):
                    act.wait_ge(early_up, FC * i + c + 1)
                    if i >= 1:
                        act.wait_ge(early_hid, FC * (i - 1) + c + 1)
                    nc.scalar.activation(gelu[c][:, :], bank_h[2 * c][:, :], ACT.Gelu).then_inc(early_gelu, 1)
                    if i == 0:
                        upper_w1(2 + c)

            nc.scalar.activation(unused[:, :], eps[:, :], ACT.Exp)
            act.wait_ge(ones_ready, 1)

            def scaled_values(t):
                nc.scalar.activation(val[:, t, 0:D], bank_h[t % 4][:, 2 * D:QKV], ACT.Copy,
                                     scale=inv2[:, t:t + 1]).then_inc(val_ready, 1)

            def early_evacuate(i):
                act.wait_ge(early_down, i + 1)
                nc.scalar.activation(y_early[:, i, :], bank_x[i][:, :], ACT.Copy).then_inc(early_y, 1)

            early_evacuate(0)
            for t in range(PRE_POOL):
                act.wait_ge(qkv_raw, t + 1)
                nc.scalar.activation(pre[:, t, :], bank_h[t % 4][:, 0:2 * D], ACT.Copy,
                                     scale=inv2[:, t:t + 1]).then_inc(scaled_ready, 1)
                scaled_values(t)
            for u in range(U):
                if 2 * u < PRE_POOL:
                    act.wait_ge(pre_ready, 2 * u + 2)
                else:
                    act.wait_ge(pre_late_ready, 2 * u + 2 - PRE_POOL)
                nc.scalar.activation(expo[:, 2 * u:2 * u + 2, :], pre[:, 2 * u:2 * u + 2, :], ACT.Exp)
                nc.scalar.activation(pre[:, 2 * u:2 * u + 2, :], pre[:, 2 * u:2 * u + 2, :],
                                     ACT.Relu).then_inc(exp_ready, 1)
                if 2 * u >= PRE_POOL:
                    scaled_values(2 * u)
                    scaled_values(2 * u + 1)
                if u == 1:
                    early_evacuate(1)
                    act.wait_ge(gap_ready, 1)
                    nc.scalar.activation(gap_exp[:, :], gap[:, :], ACT.Exp).then_inc(gap_exp_ready, 1)

            def attention_piece(kind, u):
                if kind == "queries":
                    act.wait_ge(qT_raw, u + 1)
                    nc.scalar.activation(qT[:, u * 512:(u + 1) * 512], bank_x[1][:, :],
                                         ACT.Copy).then_inc(qT_ready, 1)
                elif kind == "transposes":
                    act.wait_ge(attT_raw, u + 1)
                    if u >= 2:
                        act.wait_ge(proj_raw, u - 1)
                    nc.scalar.activation(attT[u % 2][:, :], bank_x[1][:, 0:2 * P],
                                         ACT.Copy).then_inc(attT_ready, 1)

            def split_gathered(s):
                r = steps[s][3]
                cols = steps[s][2] * P
                act.wait_ge(xg_raw, r + 1)
                if r >= 2:
                    act.wait_ge(up_done, FC * (step_of_routed[r - 2] + 1))
                nc.scalar.activation(xg_hi[r % 2][:, 0:cols], bank_x[0][:, 0:cols],
                                     ACT.Copy).then_inc(xg_hi_ready, 1)

            def evacuate(s):
                r = steps[s][3]
                if r is None:
                    return
                nj = steps[s][2]
                act.wait_ge(down_done, s + 1)
                n = (steps[s][0] - DENSE) * ST + steps[s][1]
                nc.scalar.activation(gathered[:, n:n + nj, :],
                                     bank_y[:, 0:nj * P].rearrange("p (j d) -> p j d", d=D),
                                     ACT.Copy).then_inc(y_evac, 1)

            act.wait_ge(early_hid, FC * EARLY)
            if steps[0][3] is not None:
                split_gathered(0)
            nc.scalar.activation(unused_gelu[:, :], eps[:, :], ACT.Gelu)
            for s in range(S):
                cols = steps[s][2] * P
                for c in range(FC):
                    i = FC * s + c
                    for piece in pieces_at.get((s, c, 0), []):
                        attention_piece(*piece)
                    act.wait_ge(up_done, i + 1)
                    if i >= 2:
                        act.wait_ge(hid_ready, i - 1)
                    nc.scalar.activation(gelu[i % 2][:, 0:cols], bank_h[2 * c][:, 0:cols],
                                         ACT.Gelu).then_inc(gelu_ready, 1)
                    if c == 0 and s + 1 < S and steps[s + 1][3] is not None:
                        split_gathered(s + 1)
                    for piece in pieces_at.get((s, c, 1), []):
                        attention_piece(*piece)
                    if c == 0 and s == hurried:
                        evacuate(s - 1)
                if s >= 1 and s != hurried:
                    evacuate(s - 1)
            evacuate(S - 1)
            for piece in pieces_at.get("end", []):
                attention_piece(*piece)
            act.wait_ge(gates_ready, TOP_K)
            for g in range(G):
                act.wait_ge(fetched_in[g], 16 * TOP_K)
                for k in range(TOP_K):
                    for t in range(g * GROUP + 1, (g + 1) * GROUP, 2):
                        ins = nc.scalar.activation(fetched[:, k, t, :], fetched[:, k, t, :], ACT.Copy,
                                                   scale=gate_routed[k][:, t:t + 1])
                    ins.then_inc(weighted_ready, 1)

        @block.vector
        def _(dve):
            count = [0]

            def link(ins):
                count[0] += 1
                ins.then_inc(dve_step, 1)
                dve.wait_ge(dve_step, count[0])

            nc.vector.memset(eps[:], LN_EPS).then_inc(eps_ready, 1)
            nc.vector.memset(val[:, :, D:D + 2], 1.0)

            def statistics(g):
                dve.wait_ge(x_in[g], 16)
                for t in range(g * GROUP, (g + 1) * GROUP):
                    ins = nc.vector.bn_stats(stats[:, t, :], xs[:, t, :])
                link(ins)
                for t in range(g * GROUP, (g + 1) * GROUP):
                    ins = nc.vector.bn_aggr(mv[:, t, :], stats[:, t, :])
                ins.then_inc(mv_ready, 1)

            def normalise(g):
                t0, t1 = g * GROUP, (g + 1) * GROUP
                dve.wait_ge(std1_ready, g + 1)
                link(nc.vector.reciprocal(inv1[:, t0:t1], std1[:, t0:t1]))
                nc.vector.scalar_tensor_tensor(nmi[:, t0:t1], mv[:, t0:t1, 0], -1.0, inv1[:, t0:t1],
                                               ALU.mult, ALU.mult).then_inc(nmi_ready, 1)
                for t in range(t0, t0 + 2):
                    ins = nc.vector.tensor_scalar(xn[:, t, :], xs[:, t, :], mv[:, t, 0:1], inv1[:, t:t + 1],
                                                  ALU.subtract, ALU.mult)
                ins.then_inc(xn_ready, 1)

            statistics(0)
            statistics(1)
            normalise(0)
            statistics(2)
            normalise(1)
            dve.wait_ge(small_in, 16 * 5)
            nc.vector.tensor_copy(beta_cols, beta_sb[:, 0:1].broadcast_to((P, P))).then_inc(wsmall_ready, 1)
            statistics(3)
            normalise(2)
            normalise(3)
            link(nc.vector.tensor_tensor(var2[:, :], mv[:, :, 1], inv1[:, :], ALU.mult))
            nc.vector.tensor_tensor(var2[:, :], var2[:, :], inv1[:, :], ALU.mult).then_inc(var2_ready, 1)

            def first_sum(g):
                dve.wait_ge(xn_ready, g + 1)
                dve.wait_ge(xn_act_ready, g + 1)
                nc.vector.tensor_tensor(acc[:, g * GROUP:(g + 1) * GROUP, :], xs[:, g * GROUP:(g + 1) * GROUP, :],
                                        xn[:, g * GROUP:(g + 1) * GROUP, :], ALU.add).then_inc(acc_ready, 1)

            for g in range(G - 1):
                first_sum(g)
            dve.wait_ge(std2_ready, 1)
            nc.vector.reciprocal(inv2[:, :], std2[:, :]).then_inc(ones_ready, 1)
            link(nc.vector.tensor_scalar(wqkv_g, wqkv_sb[:, :], gamma_sb[:, 0:1], None, ALU.mult))
            link(nc.vector.tensor_copy(wqkv_hi[:, :], wqkv_g))
            nc.vector.tensor_tensor(wqkv_lo[:, :], wqkv_g, wqkv_hi[:, :].bitcast(F32),
                                    ALU.subtract).then_inc(wsmall_ready, 1)

            first_sum(G - 1)
            for g in range(LO_EARLY, G):
                dve.wait_ge(xT_hi_ready, g + 1)
                nc.vector.tensor_tensor(xT_lo[:, g * 512:(g + 1) * 512], xT[:, g * 512:(g + 1) * 512],
                                        xT_hi[:, g * 512:(g + 1) * 512].bitcast(F32),
                                        ALU.subtract).then_inc(xT_late_ready, 1)

            def over_experts(ap):
                return ap.unsqueeze(2).broadcast_to((P, T, E))

            dve.wait_ge(const_ready, 1)
            dve.wait_ge(logits_ready, 1)
            scores = logits = bank_y[:, 0:T * E].rearrange("p (t e) -> p t e", e=E)
            for k in range(TOP_K):
                link(nc.vector.tensor_reduce(top[k][:, :], scores, AX.X, ALU.max))
                link(nc.vector.tensor_tensor(eq[:, :, :], scores, over_experts(top[k][:, :]), ALU.is_equal))
                link(nc.vector.tensor_tensor(eq[:, :, :], eq[:, :, :], rank[:, :, :], ALU.mult))
                link(nc.vector.tensor_reduce(best[:, :], eq[:, :, :], AX.X, ALU.max))
                link(nc.vector.tensor_tensor(chosen[:, k, :, :], eq[:, :, :], over_experts(best[:, :]), ALU.is_equal))
                if k == 0:
                    link(nc.vector.scalar_tensor_tensor(rest[:, :, :], chosen[:, 0, :, :], -3e38, logits,
                                                        ALU.mult, ALU.add))
                    scores = rest[:, :, :]
            nc.vector.tensor_tensor(assigned[:, :, :], chosen[:, 0, :, :], chosen[:, 1, :, :],
                                    ALU.add).then_inc(assigned_ready, 1)
            nc.vector.tensor_tensor(gap[:, :], top[1][:, :], top[0][:, :], ALU.subtract).then_inc(gap_ready, 1)

            def early_hidden(i):
                for c in range(FC):
                    dve.wait_ge(early_gelu, FC * i + c + 1)
                    nc.vector.tensor_tensor(hid[i % 2][:, c, :], gelu[c][:, :], bank_h[2 * c + 1][:, :],
                                            ALU.mult).then_inc(early_hid, 1)

            early_hidden(0)
            dve.wait_ge(before_ready, 1)
            before = bank_y[:, 128:128 + T * E].rearrange("p (t e) -> p t e", e=E)
            nc.vector.tensor_scalar(drop[:, :, :], before, float(CAP), DROPPED, ALU.is_ge, ALU.mult)
            link(nc.vector.tensor_tensor(slot_all[:, :, :], before, first_slot[:, :, :], ALU.add))
            link(nc.vector.tensor_tensor(slot_all[:, :, :], slot_all[:, :, :], drop[:, :, :], ALU.add))
            link(nc.vector.tensor_tensor(picked[:, :, :, :].rearrange("p k t e -> p k (t e)"),
                                         chosen[:, :, :, :].rearrange("p k t e -> p k (t e)"),
                                         slot_all[:, :, :].rearrange("p t e -> p (t e)").unsqueeze(1).broadcast_to((P, TOP_K, T * E)),
                                         ALU.mult))
            link(nc.vector.tensor_reduce(slot[:, :, :], picked[:, :, :, :], AX.X, ALU.add))
            link(nc.vector.tensor_copy(slot_i[:, :, :], slot[:, :, :]))
            nc.vector.tensor_scalar(tile_i[:, :, :], slot_i[:, :, :], 7, None, ALU.arith_shift_right)
            link(nc.vector.tensor_scalar(row_i[:, :, :], slot_i[:, :, :], P - 1, None, ALU.bitwise_and))
            nc.vector.tensor_copy(tile_16[:, :, :], tile_i[:, :, :])
            link(nc.vector.tensor_copy(row_16[:, :, :], row_i[:, :, :]))
            early_hidden(1)
            link(nc.vector.tensor_tensor(hot_tile,
                                         tile_16[:, :, :].rearrange("p k t -> p (k t)").unsqueeze(1).broadcast_to((P, RT, KT)),
                                         iota_tiles[:, :, :], ALU.is_equal))
            nc.vector.tensor_tensor(hot_token, hot_tile,
                                    token_id[:, :, :].rearrange("p k t -> p (k t)").unsqueeze(1).broadcast_to((P, RT, KT)),
                                    ALU.mult)

            def queries_keys(t):
                dve.wait_ge(qkv_raw, t + 1)
                nc.vector.scalar_tensor_tensor(pre[:, t, :], bank_h[t % 4][:, 0:2 * D], inv2[:, t:t + 1],
                                               bias[:, 0:2 * D], ALU.mult, ALU.add).then_inc(pre_late_ready, 1)

            dve.wait_ge(bias_ready, 1)
            nc.vector.tensor_tensor(hot_row[:, :, :],
                                    row_16[:, :, :].rearrange("p k t -> p (k t)").unsqueeze(1).broadcast_to((P, P, KT)),
                                    iota_rows[:, :, :], ALU.is_equal).then_inc(hot_ready, 1)
            nc.vector.tensor_scalar(kept_routed[:, :, :], slot[:, :, :], float(R * CAP), None, ALU.is_lt)
            nc.vector.tensor_scalar(kept[:, :, :], before, float(CAP), None, ALU.is_lt)

            def elu(u):
                dve.wait_ge(exp_ready, u + 1)
                nc.vector.scalar_tensor_tensor(pre[:, 2 * u:2 * u + 2, :], expo[:, 2 * u:2 * u + 2, :], 1.0,
                                               pre[:, 2 * u:2 * u + 2, :], ALU.min, ALU.add).then_inc(qk_ready, 1)

            for t in range(PRE_POOL, T):
                if t == PRE_POOL + LIST_AT:
                    dve.wait_ge(slots_ready, 1)
                    nc.vector.tensor_copy(slot_token[:, :], bank_a[:, 384:384 + RT]).then_inc(list_ready, 1)
                queries_keys(t)
                if t % 2 == 1:
                    elu((t - PRE_POOL) // 2)
            for u in range((T - PRE_POOL) // 2, U):
                elu(u)

            sums = [0]

            def before_sum(tiles):
                if sums[0] == 0:
                    dve.wait_ge(acc_ready, G)
                elif earlier_sum(sums[0], tiles):
                    dve.wait_ge(acc_added, earlier_sum(sums[0], tiles))
                sums[0] += 1

            def add_fetched(t, k):
                if t % GROUP == 0 and k == 0:
                    dve.wait_ge(fetched_in[t // GROUP], 16 * TOP_K)
                before_sum((t,))
                nc.vector.scalar_tensor_tensor(acc[:, t, :], fetched[:, k, t, :], gate_routed[k][:, t:t + 1],
                                               acc[:, t, :], ALU.mult, ALU.add).then_inc(acc_added, 1)

            def attention_piece(kind, u):
                if kind == "numerators":
                    dve.wait_ge(att_raw, u + 1)
                    both = bank_a[:, 0:2 * KVW].rearrange("p (t c) -> p t c", t=2)
                    link(nc.vector.tensor_scalar(den[:, :, :], both[:, :, D:KVW], DENOM_EPS, None, ALU.add))
                    link(nc.vector.reciprocal(den_inv[:, :, :], den[:, :, :]))
                    if u >= 2:
                        dve.wait_ge(attT_raw, u - 1)
                    nc.vector.tensor_tensor(
                        att[u % 2][:, :, :].rearrange("p t (h c) -> p t h c", h=HEADS),
                        both[:, :, 0:D].rearrange("p t (h c) -> p t h c", h=HEADS),
                        den_inv[:, :, :].unsqueeze(3).broadcast_to((P, 2, HEADS, HD)), ALU.mult).then_inc(att_ready, 1)
                elif kind == "projection":
                    dve.wait_ge(proj_raw, u + 1)
                    before_sum((2 * u, 2 * u + 1))
                    nc.vector.tensor_tensor(acc[:, 2 * u:2 * u + 2, :], acc[:, 2 * u:2 * u + 2, :],
                                            bank_x[0][:, 0:2 * D].rearrange("p (t d) -> p t d", t=2),
                                            ALU.add).then_inc(acc_added, 1)

            def add_early(i):
                e, t0, nt, _ = all_token_steps[i]
                dve.wait_ge(early_y, i + 1)
                for j in range(nt):
                    before_sum((t0 + j,))
                    nc.vector.scalar_tensor_tensor(
                        acc[:, t0 + j, :], y_early[:, i, j * D:(j + 1) * D], gate_dense[:, t0 + j, e:e + 1],
                        acc[:, t0 + j, :], ALU.mult, ALU.add).then_inc(acc_added, 1)

            def states():
                dve.wait_ge(kv_added, B)
                for b in range(B):
                    kv = bank_y[:, b * (D + 2):(b + 1) * (D + 2)]
                    link(nc.vector.tensor_scalar(v_bias[b], bias[:, 2 * D:QKV], kv[:, D:D + 1], None, ALU.mult))
                    link(nc.vector.tensor_tensor(v_bias[b], v_bias[b], kv[:, 0:D], ALU.add))
                    nc.vector.tensor_tensor(state[b][:, 0:D], v_bias[b], head_block[:, :], ALU.mult)
                    nc.vector.tensor_scalar(state[b][:, D:KVW], head_cols[:, :], kv[:, D:D + 1], None,
                                            ALU.mult).then_inc(state_ready, 1)

            def targets():
                dve.wait_ge(slots_ready, 2)
                held, second = bank_a[:, 384 + RT:384 + 2 * RT], bank_a[:, 384 + 2 * RT:384 + 3 * RT]
                nc.vector.scalar_tensor_tensor(vacant[:, :], held, 0.0, no_token[:, :], ALU.is_equal, ALU.mult)
                nc.vector.tensor_copy(choices[:, :], held)
                link(nc.vector.tensor_copy(target[:, :], bank_a[:, 384:384 + RT]))
                link(nc.vector.tensor_tensor(choices[:, :], choices[:, :], second, ALU.add))
                link(nc.vector.scalar_tensor_tensor(target[:, :], choices[:, :], float(N), target[:, :], ALU.mult, ALU.add))
                nc.vector.scalar_tensor_tensor(slot_target[:, :], target[:, :], -float(N), vacant[:, :],
                                               ALU.add, ALU.add).then_inc(target_ready, 1)

            def gates():
                dve.wait_ge(gap_exp_ready, 1)
                link(nc.vector.tensor_scalar(gate_sum[:, :], gap_exp[:, :], 1.0, None, ALU.add))
                link(nc.vector.reciprocal(gate[0][:, :], gate_sum[:, :]))
                link(nc.vector.tensor_tensor(gate[1][:, :], gate[0][:, :], gap_exp[:, :], ALU.mult))
                for k in range(TOP_K):
                    nc.vector.tensor_tensor(gate_routed[k][:, :], gate[k][:, :], kept_routed[:, k, :],
                                            ALU.mult).then_inc(gates_ready, 1)
                link(nc.vector.tensor_tensor(gate_dense[:, :, :], chosen[:, 0, :, :], over_experts(gate[0][:, :]), ALU.mult))
                link(nc.vector.tensor_tensor(gate_part[:, :, :], chosen[:, 1, :, :], over_experts(gate[1][:, :]), ALU.mult))
                link(nc.vector.tensor_tensor(gate_dense[:, :, :], gate_dense[:, :, :], gate_part[:, :, :], ALU.add))
                link(nc.vector.tensor_tensor(gate_dense[:, :, :], gate_dense[:, :, :], kept[:, :, :], ALU.mult))

            def split_gathered(s):
                r = steps[s][3]
                cols = steps[s][2] * P
                dve.wait_ge(xg_hi_ready, r + 1)
                nc.vector.tensor_tensor(xg_lo[r % 2][:, 0:cols], bank_x[0][:, 0:cols],
                                        xg_hi[r % 2][:, 0:cols].bitcast(F32),
                                        ALU.subtract).then_inc(xg_lo_ready, 1)

            def add_dense(s):
                e, t0, nt, r = steps[s]
                if r is not None:
                    return
                dve.wait_ge(down_done, s + 1)
                for j in range(nt):
                    before_sum((t0 + j,))
                    nc.vector.scalar_tensor_tensor(
                        acc[:, t0 + j, :], bank_y[:, j * D:(j + 1) * D], gate_dense[:, t0 + j, e:e + 1],
                        acc[:, t0 + j, :], ALU.mult, ALU.add).then_inc(acc_added, 1)

            if steps[0][3] is not None:
                split_gathered(0)
            dve.wait_ge(early_down, EARLY)
            for s in range(S):
                cols = steps[s][2] * P
                for c in range(FC):
                    i = FC * s + c
                    for piece in pieces_at.get((s, c, 0), []):
                        attention_piece(*piece)
                    dve.wait_ge(gelu_ready, i + 1)
                    if c == 0 and s >= 2:
                        dve.wait_ge(down_done, s - 1)
                    nc.vector.tensor_tensor(hid[s % 2][:, c, 0:cols], gelu[i % 2][:, 0:cols],
                                            bank_h[2 * c + 1][:, 0:cols], ALU.mult).then_inc(hid_ready, 1)
                    if c == 0 and s + 1 < S and steps[s + 1][3] is not None:
                        split_gathered(s + 1)
                    if (s, c) == (0, 0):
                        states()
                    if (s, c) == (0, 1):
                        targets()
                    if (s, c) == (1, 1):
                        gates()
                    if c == 0 and EARLY_SUMS <= s < EARLY_SUMS + EARLY:
                        add_early(s - EARLY_SUMS)
                    for piece in pieces_at.get((s, c, 1), []):
                        attention_piece(*piece)
                if s >= 1:
                    add_dense(s - 1)
            for piece in pieces_at.get("end", []):
                attention_piece(*piece)
            for t in range(0, T, 2):
                if t == T - GROUP:
                    add_dense(S - 1)
                for k in range(TOP_K):
                    add_fetched(t, k)

        @block.tensor
        def _(pe):
            def product(dst, halves):
                (a_hi, a_lo), (b_hi, b_lo) = halves
                nc.tensor.matmul(dst, a_lo, b_hi, start=True, stop=False)
                nc.tensor.matmul(dst, a_hi, b_lo, start=False, stop=False)
                return nc.tensor.matmul(dst, a_hi, b_hi, start=False, stop=True)

            def x_halves(t):
                return xT_hi[:, t * P:(t + 1) * P], xT_lo[:, t * P:(t + 1) * P]

            def transpose_group(g):
                pe.wait_ge(xn_ready, g + 1)
                pe.wait_ge(xn_act_ready, g + 1)
                if g >= 2:
                    pe.wait_ge(xT_ready, g - 1)
                for j in range(GROUP):
                    ins = nc.tensor.transpose(bank_x[g % 2][:, j * P:(j + 1) * P], xn[:, g * GROUP + j, :],
                                              ident[:, :])
                ins.then_inc(xT_raw, 1)

            def logits_group(g):
                pe.wait_ge(xT_ready, g + 1)
                for t in range(g * GROUP, (g + 1) * GROUP):
                    ins = nc.tensor.matmul(bank_y[:, t * E:(t + 1) * E], xT[:, t * P:(t + 1) * P], wg_sb[:, :],
                                           start=True, stop=True)
                if g == G - 1:
                    ins.then_inc(logits_ready, 1)

            pe.wait_ge(ident_ready, 1)
            transpose_group(0)
            transpose_group(1)
            pe.wait_ge(wsmall_ready, 1)
            logits_group(0)
            transpose_group(2)
            logits_group(1)
            transpose_group(3)
            logits_group(2)
            logits_group(3)
            nc.tensor.matmul(bank_a[:, 0:QKV], beta_cols, wqkv_sb[:, :],
                             start=True, stop=True).then_inc(bias_raw, 1)

            def qkv_tile(t):
                g = t // GROUP
                if g < LO_EARLY:
                    pe.wait_ge(xT_lo_ready, g + 1)
                else:
                    pe.wait_ge(xT_late_ready, g - LO_EARLY + 1)
                if t >= 4:
                    pe.wait_ge(val_ready, t - 3)
                product(bank_h[t % 4][:, 0:QKV], (x_halves(t), (wqkv_hi[:, :], wqkv_lo[:, :]))).then_inc(qkv_raw, 1)

            def early_products(i):
                e, t0, _, _ = all_token_steps[i]
                pe.wait_ge(w1_lo_ready, e + 1)
                g = t0 // GROUP
                if g < LO_EARLY:
                    pe.wait_ge(xT_lo_ready, g + 1)
                else:
                    pe.wait_ge(xT_late_ready, g - LO_EARLY + 1)
                right = xT_hi[:, t0 * P:(t0 + GROUP) * P], xT_lo[:, t0 * P:(t0 + GROUP) * P]
                for c in range(FC):
                    if i >= 1:
                        pe.wait_ge(early_gelu, FC * (i - 1) + c + 1)
                        pe.wait_ge(early_hid, FC * (i - 1) + c + 1)
                    for h, first in enumerate((c * P, F + c * P)):
                        left = w1_hi[:, e, first:first + P], w1_lo[:, e, first:first + P]
                        ins = product(bank_h[2 * c + h][:, :], (left, right))
                    ins.then_inc(early_up, 1)

            def early_results(i):
                e = all_token_steps[i][0]
                pe.wait_ge(early_hid, FC * (i + 1))
                pe.wait_ge(w2_in[min(e // 2, 1)], 16)
                for j in range(GROUP):
                    for c in range(FC):
                        ins = nc.tensor.matmul(bank_x[i][:, j * D:(j + 1) * D], hid[i][:, c, j * P:(j + 1) * P],
                                               w2_sb[:, e, c, :], start=(c == 0), stop=(c == FC - 1))
                ins.then_inc(early_down, 1)

            early_products(0)
            pe.wait_ge(const_ready, 1)
            pe.wait_ge(assigned_ready, 1)
            before = bank_y[:, 128:128 + T * E]
            nc.tensor.matmul(before, earlier[:, :], assigned[:, :, :], start=True, stop=False)
            for t in range(T - 1):
                ins = nc.tensor.matmul(before[:, (t + 1) * E:].rearrange("p (t e) -> p t e", e=E), ones_bf[:, :],
                                       assigned[:, t:t + 1, :].broadcast_to((P, T - 1 - t, E)),
                                       start=False, stop=(t == T - 2))
            ins.then_inc(before_ready, 1)
            early_products(1)
            pe.wait_ge(xT_ready, G)
            early_results(0)
            pe.wait_ge(wsmall_ready, 2)
            pe.wait_ge(early_gelu, FC * EARLY)
            pe.wait_ge(early_hid, FC * EARLY)
            for t in range(SLOTS_AT):
                if t == RESULTS_AT:
                    early_results(1)
                qkv_tile(t)
            pe.wait_ge(bias_ready, 1)
            pe.wait_ge(hot_ready, 1)
            for n in range(KT):
                ins = nc.tensor.matmul(bank_a[:, 384:384 + 2 * RT], hot_row[:, :, n], hot[:, :, n],
                                       start=(n == 0), stop=(n == KT - 1))
            ins.then_inc(slots_ready, 1)

            def kv_tile(t):
                b = t // TB
                if t == 0:
                    pe.wait_ge(list_ready, 1)
                pe.wait_ge(qk_ready, t // 2 + 1)
                pe.wait_ge(val_ready, t + 1)
                ins = nc.tensor.matmul(bank_y[:, b * (D + 2):(b + 1) * (D + 2)], pre[:, t, D:2 * D], val[:, t, :],
                                       start=(t % TB == 0), stop=(t % TB == TB - 1))
                if t % TB == TB - 1:
                    ins.then_inc(kv_added, 1)

            for t in range(SLOTS_AT, T):
                qkv_tile(t)
                if t >= SLOTS_AT + 2 and t >= KV_LAG:
                    for v in range(0 if t == max(SLOTS_AT + 2, KV_LAG) else t - KV_LAG, t - KV_LAG + 1):
                        kv_tile(v)
            pe.wait_ge(list_ready, 1)
            for n in range(T, KT):
                ins = nc.tensor.matmul(bank_a[:, 384 + 2 * RT:384 + 3 * RT], hot_row[:, :, n], hot_tile[:, :, n],
                                       start=(n == T), stop=(n == KT - 1))
            ins.then_inc(slots_ready, 1)

            bank_x0_read = [(early_y, EARLY)]

            def attention_piece(kind, u):
                if kind == "queries":
                    if u >= 1:
                        pe.wait_ge(qT_ready, u)
                    else:
                        pe.wait_ge(early_y, EARLY)
                    for j in range(GROUP):
                        ins = nc.tensor.transpose(bank_x[1][:, j * P:(j + 1) * P], pre[:, u * GROUP + j, 0:D],
                                                  ident[:, :])
                    ins.then_inc(qT_raw, 1)
                elif kind == "numerators":
                    if u == 0:
                        pe.wait_ge(target_ready, 1)
                    pe.wait_ge(qT_ready, u // 2 + 1)
                    if u >= 1:
                        pe.wait_ge(att_ready, u)
                    for i in range(2):
                        t = 2 * u + i
                        ins = nc.tensor.matmul(bank_a[:, i * KVW:(i + 1) * KVW], qT[:, t * P:(t + 1) * P],
                                               state[t // TB][:, :], start=True, stop=True)
                    ins.then_inc(att_raw, 1)
                elif kind == "transposes":
                    pe.wait_ge(att_ready, u + 1)
                    if u >= 1:
                        pe.wait_ge(attT_ready, u)
                    else:
                        pe.wait_ge(qT_ready, G)
                    for i in range(2):
                        ins = nc.tensor.transpose(bank_x[1][:, i * P:(i + 1) * P], att[u % 2][:, i, :], ident[:, :])
                    ins.then_inc(attT_raw, 1)
                else:
                    pe.wait_ge(attT_ready, u + 1)
                    pe.wait_ge(*bank_x0_read[0])
                    bank_x0_read[0] = (acc_added, sums_with["projection", u])
                    for i in range(2):
                        ins = nc.tensor.matmul(bank_x[0][:, i * D:(i + 1) * D], attT[u % 2][:, i * P:(i + 1) * P],
                                               wout_sb[:, :], start=True, stop=True)
                    ins.then_inc(proj_raw, 1)

            def transpose_slots(s):
                e, j0, nj, r = steps[s]
                if j0 == 0:
                    pe.wait_ge(rows_in[e - DENSE], 16 * ST)
                pe.wait_ge(*bank_x0_read[0])
                bank_x0_read[0] = (xg_lo_ready, r + 1)
                for j in range(nj):
                    n = (e - DENSE) * ST + j0 + j
                    ins = nc.tensor.transpose(bank_x[0][:, j * P:(j + 1) * P], gathered[:, n, :], ident[:, :])
                ins.then_inc(xg_raw, 1)

            def up(s):
                e, j0, nj, r = steps[s]
                cols = nj * P
                if r is None:
                    right = xT_hi[:, j0 * P:j0 * P + cols], xT_lo[:, j0 * P:j0 * P + cols]
                else:
                    pe.wait_ge(xg_lo_ready, r + 1)
                    right = xg_hi[r % 2][:, 0:cols], xg_lo[r % 2][:, 0:cols]
                pe.wait_ge(w1_lo_ready, e + 1)
                for c in range(FC):
                    if c == 1 and s == hurried:
                        down(s - 1)
                    if c == 1 and s + 1 < S and steps[s + 1][3] is not None:
                        transpose_slots(s + 1)
                    if s >= 1:
                        pe.wait_ge(gelu_ready, FC * (s - 1) + c + 1)
                        pe.wait_ge(hid_ready, FC * (s - 1) + c + 1)
                    for i, first in enumerate((c * P, F + c * P)):
                        left = w1_hi[:, e, first:first + P], w1_lo[:, e, first:first + P]
                        ins = product(bank_h[2 * c + i][:, 0:cols], (left, right))
                        if i == 1:
                            ins.then_inc(up_done, 1)
                        for piece in pieces_at.get((s, c, i), []):
                            attention_piece(*piece)

            def down(s):
                e, _, nj, _ = steps[s]
                pe.wait_ge(hid_ready, FC * (s + 1))
                if s >= 1:
                    if steps[s - 1][3] is not None:
                        pe.wait_ge(y_evac, steps[s - 1][3] + 1)
                    else:
                        pe.wait_ge(acc_added, sums_with["step", s - 1])
                else:
                    pe.wait_ge(state_ready, B)
                pe.wait_ge(w2_in[min(e // 2, 1)], 16)
                for j in range(nj):
                    for c in range(FC):
                        ins = nc.tensor.matmul(bank_y[:, j * D:(j + 1) * D], hid[s % 2][:, c, j * P:(j + 1) * P],
                                               w2_sb[:, e, c, :], start=(c == 0), stop=(c == FC - 1))
                ins.then_inc(down_done, 1)

            transpose_slots(0)
            for t in range(T - KV_LAG, T):
                kv_tile(t)
            pe.wait_ge(val_ready, T)
            for s in range(S):
                up(s)
                if s >= 1 and s != hurried:
                    down(s - 1)
            down(S - 1)
            for piece in pieces_at.get("end", []):
                attention_piece(*piece)


def kernel(L0_attn_x, L0_attn_gamma, L0_attn_beta, L0_attn_Wqkv, L0_attn_Wout, L0_ffn_Wg, L0_ffn_W1, L0_ffn_W2):
    import numpy as np
    import concourse.bacc as bacc
    from concourse.bass_utils import run_bass_kernel_spmd

    laid_out = {
        "x": L0_attn_x,
        "gamma": np.asarray(L0_attn_gamma).reshape(-1, 1),
        "beta": np.asarray(L0_attn_beta).reshape(-1, 1),
        "wqkv": L0_attn_Wqkv,
        "wout": L0_attn_Wout,
        "wg_t": np.asarray(L0_ffn_Wg).T,
        "w1": L0_ffn_W1,
        "w2": L0_ffn_W2,
    }
    nc = bacc.Bacc("TRN2", target_bir_lowering=False, num_devices=1)
    arrays, args = {}, []
    for name, a in laid_out.items():
        a = np.ascontiguousarray(a)
        arrays[f"in_{name}"] = a
        args.append(nc.dram_tensor(f"in_{name}", a.shape, mybir.dt.from_np(a.dtype), kind="ExternalInput").ap())
    shape = np.asarray(L0_attn_x).shape
    args.append(nc.dram_tensor("out_block", shape, F32, kind="ExternalOutput").ap())
    moe_attention_block(nc, *args)
    r = run_bass_kernel_spmd(nc, [arrays], core_ids=[0])
    return r.results[0]["out_block"]
```
